# Optimizing a Trainium2 kernel written in Bass

```python
import numpy as np
import jax
import jax.numpy as jnp

def _softmax(x, axis=-1):
    return jax.nn.softmax(x, axis=axis)

def _gelu(x):
    return jax.nn.gelu(x, approximate=True)

def _silu(x):
    return jax.nn.silu(x)

def _sigmoid(x):
    return jax.nn.sigmoid(x)

def _layernorm(x, axis=-1, eps=1e-05):
    m = jnp.mean(x, axis=axis, keepdims=True)
    v = jnp.var(x, axis=axis, keepdims=True)
    return (x - m) / jnp.sqrt(v + eps)

def _scatter_add(tgt, idx, src, axis=0):
    return tgt.at[idx].add(src)

def _segment_sum(src, seg, n):
    return jax.ops.segment_sum(src, seg, n)
kernel_name = 'mk_conv_seq_d2_conv_nchw192_r2_380ab9'

def setup_inputs(seed: int=0):
    np.random.seed(seed)
    _w = jnp.asarray

    def _rec_inputs():
        import jax
        import jax.numpy as jnp
        _gk = jax.random.key(seed)
        x = -0.0001538 + 1 * jax.random.normal(jax.random.fold_in(_gk, 1), (8, 96, 32, 32), jnp.float32)
        return x
    x = _rec_inputs()

    def _L0_conv_setup():
        import jax, jax.numpy as jnp
        import numpy as np
        from jax import lax
        D_MODEL, D_STATE, D_CONV, EXPAND = (96, 16, 4, 2)
        D_INNER = EXPAND * D_MODEL
        DT_RANK = (D_MODEL + 15) // 16

        def _mamba(u, W_in, conv_w, conv_b, W_x, W_dt, b_dt, A_log, D, W_out):
            b, l, _ = u.shape
            xz = u @ W_in
            xr, z = jnp.split(xz, 2, axis=-1)
            xc = lax.conv_general_dilated(xr.transpose(0, 2, 1), conv_w, (1,), [(D_CONV - 1, 0)], dimension_numbers=('NCH', 'OIH', 'NCH'), feature_group_count=D_INNER)
            x = jax.nn.silu((xc + conv_b[None, :, None]).transpose(0, 2, 1))
            x_dbl = x @ W_x
            dt, Bm, Cm = jnp.split(x_dbl, [DT_RANK, DT_RANK + D_STATE], axis=-1)
            delta = jax.nn.softplus(dt @ W_dt + b_dt)
            A = -jnp.exp(A_log)

            def step(h, inp):
                d_t, B_t, x_t, C_t = inp
                dA = jnp.exp(d_t[..., None] * A)
                h = dA * h + (d_t * x_t)[..., None] * B_t[:, None, :]
                y = jnp.einsum('bdn,bn->bd', h, C_t)
                return (h, y)
            h0 = jnp.zeros((b, D_INNER, D_STATE), u.dtype)
            _, ys = lax.scan(step, h0, (delta.transpose(1, 0, 2), Bm.transpose(1, 0, 2), x.transpose(1, 0, 2), Cm.transpose(1, 0, 2)))
            y = ys.transpose(1, 0, 2) + x * D
            y = y * jax.nn.silu(z)
            return y @ W_out
        key = jax.random.key(seed)
        ks = jax.random.split(key, 12)
        B, C, H, W = (8, D_MODEL, 32, 32)
        s = lambda *sh: 1.0 / np.sqrt(sh[0])
        inp = {'x': jax.random.normal(ks[0], (B, C, H, W), jnp.float32), 'W_in': jax.random.normal(ks[1], (D_MODEL, 2 * D_INNER), jnp.float32) * s(D_MODEL), 'conv_w': jax.random.normal(ks[2], (D_INNER, 1, D_CONV), jnp.float32) * s(D_CONV), 'conv_b': jax.random.normal(ks[3], (D_INNER,), jnp.float32) * 0.02, 'W_x': jax.random.normal(ks[4], (D_INNER, DT_RANK + 2 * D_STATE), jnp.float32) * s(D_INNER), 'W_dt': jax.random.normal(ks[5], (DT_RANK, D_INNER), jnp.float32) * s(DT_RANK), 'b_dt': jax.random.normal(ks[6], (D_INNER,), jnp.float32) * 0.02, 'A_log': jnp.log(jnp.broadcast_to(jnp.arange(1, D_STATE + 1, dtype=jnp.float32), (D_INNER, D_STATE))), 'D': jnp.ones((D_INNER,), jnp.float32), 'W_out': jax.random.normal(ks[7], (D_INNER, D_MODEL), jnp.float32) * s(D_INNER), 'ln_g': jnp.ones((D_MODEL,), jnp.float32), 'ln_b': jnp.zeros((D_MODEL,), jnp.float32)}
        return inp
    _L0_conv_all = _L0_conv_setup()
    _L0_conv_in = {k: v for k, v in _L0_conv_all.items() if k in ('W_in', 'conv_w', 'conv_b', 'W_x', 'W_dt', 'b_dt', 'A_log', 'D', 'W_out', 'ln_g', 'ln_b')}
    del _L0_conv_all

    def _L1_conv_setup():
        import jax, jax.numpy as jnp
        import numpy as np
        DIM = 96
        D_STATE = 16
        D_CONV = 4
        EXPAND = 2
        D_INNER = EXPAND * DIM
        DT_RANK = DIM // 16

        def _silu(x):
            return x * jax.nn.sigmoid(x)

        def _causal_conv(x, w, b):
            L = x.shape[1]
            xp = jnp.pad(x, ((0, 0), (D_CONV - 1, 0), (0, 0)))
            y = sum((xp[:, k:k + L, :] * w[:, k] for k in range(D_CONV)))
            return y + b

        def _selective_scan(x, dt, Bm, Cm, A, D):
            Bsz, L, di = x.shape
            ds = A.shape[1]

            def step(h, inp):
                x_t, dt_t, B_t, C_t = inp
                dA = jnp.exp(dt_t[:, :, None] * A)
                h = dA * h + dt_t[:, :, None] * B_t[:, None, :] * x_t[:, :, None]
                y = jnp.einsum('bds,bs->bd', h, C_t)
                return (h, y)
            h0 = jnp.zeros((Bsz, di, ds), x.dtype)
            xs = (jnp.swapaxes(x, 0, 1), jnp.swapaxes(dt, 0, 1), jnp.swapaxes(Bm, 0, 1), jnp.swapaxes(Cm, 0, 1))
            _, ys = jax.lax.scan(step, h0, xs)
            return jnp.swapaxes(ys, 0, 1) + x * D

        def _mamba(x_seq, W_in, conv_w, conv_b, W_xproj, W_dt, b_dt, A_log, D, W_out):
            xz = x_seq @ W_in
            x, z = (xz[..., :D_INNER], xz[..., D_INNER:])
            x = _silu(_causal_conv(x, conv_w, conv_b))
            proj = x @ W_xproj
            dt = jax.nn.softplus(proj[..., :DT_RANK] @ W_dt + b_dt)
            Bm = proj[..., DT_RANK:DT_RANK + D_STATE]
            Cm = proj[..., DT_RANK + D_STATE:]
            A = -jnp.exp(A_log)
            y = _selective_scan(x, dt, Bm, Cm, A, D)
            return y * _silu(z) @ W_out
        key = jax.random.key(seed)
        ks = jax.random.split(key, 8)
        B, C, H, W = (4, DIM, 32, 32)
        x = jax.random.normal(ks[0], (B, C, H, W), dtype=jnp.float32)
        s_in = 1.0 / np.sqrt(DIM)
        s_xp = 1.0 / np.sqrt(D_INNER)
        s_dt = 1.0 / np.sqrt(DT_RANK)
        params = {'x': x, 'ln_g': jnp.ones((DIM,), jnp.float32), 'ln_b': jnp.zeros((DIM,), jnp.float32), 'W_in': jax.random.normal(ks[1], (DIM, 2 * D_INNER), jnp.float32) * s_in, 'conv_w': jax.random.normal(ks[2], (D_INNER, D_CONV), jnp.float32) * 0.5, 'conv_b': jnp.zeros((D_INNER,), jnp.float32), 'W_xproj': jax.random.normal(ks[3], (D_INNER, DT_RANK + 2 * D_STATE), jnp.float32) * s_xp, 'W_dt': jax.random.normal(ks[4], (DT_RANK, D_INNER), jnp.float32) * s_dt, 'b_dt': jax.random.normal(ks[5], (D_INNER,), jnp.float32) * 0.5 - 4.0, 'A_log': jnp.log(jnp.broadcast_to(jnp.arange(1, D_STATE + 1, dtype=jnp.float32), (D_INNER, D_STATE))) + 0.0, 'D': jnp.ones((D_INNER,), jnp.float32), 'W_out': jax.random.normal(ks[6], (D_INNER, DIM), jnp.float32) * s_xp}
        return params
    _L1_conv_all = _L1_conv_setup()
    _L1_conv_in = {k: v for k, v in _L1_conv_all.items() if k in ('ln_g', 'ln_b', 'W_in', 'conv_w', 'conv_b', 'W_xproj', 'W_dt', 'b_dt', 'A_log', 'D', 'W_out')}
    del _L1_conv_all
    return {'x': x, 'L0_conv_W_in': _L0_conv_in['W_in'], 'L0_conv_conv_w': _L0_conv_in['conv_w'], 'L0_conv_conv_b': _L0_conv_in['conv_b'], 'L0_conv_W_x': _L0_conv_in['W_x'], 'L0_conv_W_dt': _L0_conv_in['W_dt'], 'L0_conv_b_dt': _L0_conv_in['b_dt'], 'L0_conv_A_log': _L0_conv_in['A_log'], 'L0_conv_D': _L0_conv_in['D'], 'L0_conv_W_out': _L0_conv_in['W_out'], 'L0_conv_ln_g': _L0_conv_in['ln_g'], 'L0_conv_ln_b': _L0_conv_in['ln_b'], 'L1_conv_ln_g': _L1_conv_in['ln_g'], 'L1_conv_ln_b': _L1_conv_in['ln_b'], 'L1_conv_W_in': _L1_conv_in['W_in'], 'L1_conv_conv_w': _L1_conv_in['conv_w'], 'L1_conv_conv_b': _L1_conv_in['conv_b'], 'L1_conv_W_xproj': _L1_conv_in['W_xproj'], 'L1_conv_W_dt': _L1_conv_in['W_dt'], 'L1_conv_b_dt': _L1_conv_in['b_dt'], 'L1_conv_A_log': _L1_conv_in['A_log'], 'L1_conv_D': _L1_conv_in['D'], 'L1_conv_W_out': _L1_conv_in['W_out']}

def reference(x, L0_conv_W_in, L0_conv_conv_w, L0_conv_conv_b, L0_conv_W_x, L0_conv_W_dt, L0_conv_b_dt, L0_conv_A_log, L0_conv_D, L0_conv_W_out, L0_conv_ln_g, L0_conv_ln_b, L1_conv_ln_g, L1_conv_ln_b, L1_conv_W_in, L1_conv_conv_w, L1_conv_conv_b, L1_conv_W_xproj, L1_conv_W_dt, L1_conv_b_dt, L1_conv_A_log, L1_conv_D, L1_conv_W_out):
    import jax
    import jax.numpy as jnp

    def _L0_conv_ref(x, W_in, conv_w, conv_b, W_x, W_dt, b_dt, A_log, D, W_out, ln_g, ln_b):
        import jax, jax.numpy as jnp
        import numpy as np
        from jax import lax
        D_MODEL, D_STATE, D_CONV, EXPAND = (96, 16, 4, 2)
        D_INNER = EXPAND * D_MODEL
        DT_RANK = (D_MODEL + 15) // 16

        def _mamba(u, W_in, conv_w, conv_b, W_x, W_dt, b_dt, A_log, D, W_out):
            b, l, _ = u.shape
            xz = u @ W_in
            xr, z = jnp.split(xz, 2, axis=-1)
            xc = lax.conv_general_dilated(xr.transpose(0, 2, 1), conv_w, (1,), [(D_CONV - 1, 0)], dimension_numbers=('NCH', 'OIH', 'NCH'), feature_group_count=D_INNER)
            x = jax.nn.silu((xc + conv_b[None, :, None]).transpose(0, 2, 1))
            x_dbl = x @ W_x
            dt, Bm, Cm = jnp.split(x_dbl, [DT_RANK, DT_RANK + D_STATE], axis=-1)
            delta = jax.nn.softplus(dt @ W_dt + b_dt)
            A = -jnp.exp(A_log)

            def step(h, inp):
                d_t, B_t, x_t, C_t = inp
                dA = jnp.exp(d_t[..., None] * A)
                h = dA * h + (d_t * x_t)[..., None] * B_t[:, None, :]
                y = jnp.einsum('bdn,bn->bd', h, C_t)
                return (h, y)
            h0 = jnp.zeros((b, D_INNER, D_STATE), u.dtype)
            _, ys = lax.scan(step, h0, (delta.transpose(1, 0, 2), Bm.transpose(1, 0, 2), x.transpose(1, 0, 2), Cm.transpose(1, 0, 2)))
            y = ys.transpose(1, 0, 2) + x * D
            y = y * jax.nn.silu(z)
            return y @ W_out
        B, C, H, W = x.shape
        seq = x.transpose(0, 2, 3, 1).reshape(B * H, W, C)
        y = _mamba(seq, W_in, conv_w, conv_b, W_x, W_dt, b_dt, A_log, D, W_out)
        y = y.reshape(B, H, W, C)
        mu = y.mean(-1, keepdims=True)
        var = y.var(-1, keepdims=True)
        y = (y - mu) * lax.rsqrt(var + 1e-05) * ln_g + ln_b
        return y.transpose(0, 3, 1, 2)

    def _L1_conv_ref(x, ln_g, ln_b, W_in, conv_w, conv_b, W_xproj, W_dt, b_dt, A_log, D, W_out):
        import jax, jax.numpy as jnp
        import numpy as np
        DIM = 96
        D_STATE = 16
        D_CONV = 4
        EXPAND = 2
        D_INNER = EXPAND * DIM
        DT_RANK = DIM // 16

        def _silu(x):
            return x * jax.nn.sigmoid(x)

        def _causal_conv(x, w, b):
            L = x.shape[1]
            xp = jnp.pad(x, ((0, 0), (D_CONV - 1, 0), (0, 0)))
            y = sum((xp[:, k:k + L, :] * w[:, k] for k in range(D_CONV)))
            return y + b

        def _selective_scan(x, dt, Bm, Cm, A, D):
            Bsz, L, di = x.shape
            ds = A.shape[1]

            def step(h, inp):
                x_t, dt_t, B_t, C_t = inp
                dA = jnp.exp(dt_t[:, :, None] * A)
                h = dA * h + dt_t[:, :, None] * B_t[:, None, :] * x_t[:, :, None]
                y = jnp.einsum('bds,bs->bd', h, C_t)
                return (h, y)
            h0 = jnp.zeros((Bsz, di, ds), x.dtype)
            xs = (jnp.swapaxes(x, 0, 1), jnp.swapaxes(dt, 0, 1), jnp.swapaxes(Bm, 0, 1), jnp.swapaxes(Cm, 0, 1))
            _, ys = jax.lax.scan(step, h0, xs)
            return jnp.swapaxes(ys, 0, 1) + x * D

        def _mamba(x_seq, W_in, conv_w, conv_b, W_xproj, W_dt, b_dt, A_log, D, W_out):
            xz = x_seq @ W_in
            x, z = (xz[..., :D_INNER], xz[..., D_INNER:])
            x = _silu(_causal_conv(x, conv_w, conv_b))
            proj = x @ W_xproj
            dt = jax.nn.softplus(proj[..., :DT_RANK] @ W_dt + b_dt)
            Bm = proj[..., DT_RANK:DT_RANK + D_STATE]
            Cm = proj[..., DT_RANK + D_STATE:]
            A = -jnp.exp(A_log)
            y = _selective_scan(x, dt, Bm, Cm, A, D)
            return y * _silu(z) @ W_out
        B, C, H, W = x.shape
        xh = jnp.transpose(x, (0, 2, 3, 1))
        mu = xh.mean(-1, keepdims=True)
        var = xh.var(-1, keepdims=True)
        xn = (xh - mu) * jax.lax.rsqrt(var + 1e-05) * ln_g + ln_b
        x_seq = xn.reshape(B, H * W, C)
        mparams = (W_in, conv_w, conv_b, W_xproj, W_dt, b_dt, A_log, D, W_out)
        out_fwd = _mamba(x_seq, *mparams)
        out_bwd = jnp.flip(_mamba(jnp.flip(x_seq, 1), *mparams), 1)
        out = out_fwd + out_bwd
        return jnp.transpose(out, (0, 2, 1)).reshape(B, C, H, W)

    def _gn(v, G=32, eps=1e-05):
        B_, C_, H_, W_ = v.shape
        g = v.reshape(B_, G, C_ // G, H_, W_)
        m = jnp.mean(g, axis=(2, 3, 4), keepdims=True)
        s = jnp.var(g, axis=(2, 3, 4), keepdims=True)
        return ((g - m) / jnp.sqrt(s + eps)).reshape(v.shape)

    def _ln_c(v, eps=1e-06):
        m = jnp.mean(v, axis=1, keepdims=True)
        s = jnp.var(v, axis=1, keepdims=True)
        return (v - m) / jnp.sqrt(s + eps)

    def _ln_t(v, eps=1e-05):
        m = jnp.mean(v, axis=-1, keepdims=True)
        s = jnp.var(v, axis=-1, keepdims=True)
        return (v - m) / jnp.sqrt(s + eps)

    def _to_tokens(v):
        B_, C_, H_, W_ = v.shape
        return v.reshape(B_, C_, H_ * W_).transpose(0, 2, 1)

    def _from_tokens(t, like):
        B_, C_, H_, W_ = like.shape
        return t.transpose(0, 2, 1).reshape(B_, C_, H_, W_)
    x = _L0_conv_ref(x, L0_conv_W_in, L0_conv_conv_w, L0_conv_conv_b, L0_conv_W_x, L0_conv_W_dt, L0_conv_b_dt, L0_conv_A_log, L0_conv_D, L0_conv_W_out, L0_conv_ln_g, L0_conv_ln_b)
    x = _L1_conv_ref(x, L1_conv_ln_g, L1_conv_ln_b, L1_conv_W_in, L1_conv_conv_w, L1_conv_conv_b, L1_conv_W_xproj, L1_conv_W_dt, L1_conv_b_dt, L1_conv_A_log, L1_conv_D, L1_conv_W_out)
    return x

_drawn_inputs = setup_inputs


def setup_inputs(seed=0):
    import zlib

    import numpy as np

    out = dict(_drawn_inputs(seed))
    spreads = {'L0_conv_D': (1.0, 0.2),
     'L0_conv_ln_g': (1.0, 0.2),
     'L0_conv_ln_b': (0.0, 0.1),
     'L1_conv_ln_g': (1.0, 0.2),
     'L1_conv_ln_b': (0.0, 0.1),
     'L1_conv_conv_b': (0.0, 0.1),
     'L1_conv_D': (1.0, 0.2)}
    factors = {'L0_conv_b_dt': 2.691}
    for name, (base, spread) in spreads.items():
        noise = np.random.default_rng([zlib.crc32(name.encode()), seed]).standard_normal(out[name].shape)
        drawn = base * np.exp(spread * noise) if base else spread * noise
        out[name] = jnp.asarray(drawn.astype(out[name].dtype))
    for name, factor in factors.items():
        out[name] = (out[name] * factor).astype(out[name].dtype)
    return out
```

```python
import numpy as np
import concourse.bass as bass
from concourse import mybir
from contextlib import ExitStack

B, C, H, W = 8, 96, 32, 32
T = H * W
DI = 2 * C
NS = 16
RANK = C // 16
TAPS = 4
P = 128
DM = DI - P
PAIRS = B // 2
HALF = T // 2
BIG = 1.0e34
LN_CAP = 1.0e13
EPS = 1e-5

ROWS, FWD, BWD = "rows", "fwd", "bwd"
LAYER = {ROWS: 0, FWD: 1, BWD: 1}
TILES = 3
STEPS = TILES * NS
RING = 4

_cols, _at = {}, 0
for _name, _n in [("w_xr", 3 * P), ("w_z", 3 * P), ("w_dbl", 3 * P), ("w_dt", 3 * P), ("w_out", 3 * C),
                  ("small", 2 * 7), ("a_log", 2 * NS)]:
    for _layer in range(2):
        _cols[_name, _layer] = (_at, _n)
        _at += _n
for _name, _n in [("ident", P), ("mean", C), ("sel", 2 * NS), ("split", 2), ("ln", 4)]:
    _cols[_name, None] = (_at, _n)
    _at += _n
NCOL = _at


def fills_prep(kind, pair, first=0):
    out = []
    for u in range(6):
        out.append((u, "xr", u))
    for k in range(TILES):
        for m in range(TAPS - 1):
            out.append((2 + 2 * k + m, "conv", 3 * k + m))
        for j in range(2):
            out.append((5 + 2 * k + j, "tanh", 2 * k + j))
            out.append((6 + 2 * k + j, "silu", 2 * k + j))
        out.append((10 + k, "skip", k))
    for c in range(4):
        out.append((12 + c, "dbl", c))
        out.append((13 + c, "split_hi", c))
        out.append((14 + c, "split_mid", c))
        out.append((15 + c, "split_lo", c))
        out.append((16 + c, "bc_in", c))
    for n, u in enumerate((0, 1, 4, 5)):
        out.append((17 + n, "dt", u))
    for u in (2, 3):
        out.append((31 + u, "dt", u))
    for k, at in ((0, (19, 23, 24, 25)), (2, (21, 23, 25, 27)), (1, (35, 37, 38, 39))):
        out += [(at[0], "dt_cap", k), (at[1], "dt_ln", k), (at[2], "dt_max", k), (at[3], "u", k)]
    if kind != BWD:
        for u in range(6):
            out.append((38 + u, "z", u))
            out.append((39 + u, "gate", u))
    return [(s, name, kind, pair, i) for s, name, i in sorted(out, key=lambda x: x[0])]


def fills_post(kind, pair):
    out = [(0, "gated", 0), (1, "gated", 1), (4, "gated", 2)]
    for c in range(4):
        out.append((6 + c - (kind == ROWS), "w_out", c))
    if kind == ROWS:
        for c in range(4):
            out.append((9 + c, "mean", c))
            out.append((11 + c, "square", c))
            out.append((13 + c, "var", c))
            out.append((28 + 2 * (c // 2), "mean", 4 + c))
            out.append((29 + 2 * (c // 2), "square", 4 + c))
            out.append((30 + c, "var", 4 + c))
        for r, at in ((0, (23, 25, 27)), (1, (37, 39, 41))):
            out.append((at[0], "rstd", r))
            for b in range(2):
                out.append((at[1] + 2 * b, "norm", 2 * r + b))
                out.append((at[2] + 2 * b, "affine", 2 * r + b))
    return [(s, name, kind, pair, i) for s, name, i in sorted(out, key=lambda x: x[0])]


BANKED = {"xr", "z", "dbl", "dt", "w_out", "mean", "var"}


def plan():
    def item(kind, pair, *fills, drain=False):
        slots = [[] for _ in range(STEPS)]
        for f in fills:
            for s, *job in f:
                slots[s].append(tuple(job))
        return {"kind": kind, "pair": pair, "slots": slots, "drain": drain}

    def alone(*fills):
        jobs = sorted((x for f in fills for x in f), key=lambda x: x[0])
        return {"kind": None, "slots": [[tuple(x[1:]) for x in jobs]]}

    load = lambda pair, slot: [(slot, "load", ROWS, pair, 0)]
    parts = [
        alone(load(0, -1), fills_prep(ROWS, 0)),
        item(ROWS, 0, load(1, 0), [(s + 1 if s < 3 else s, *r) for s, *r in fills_prep(ROWS, 1)], drain=True),
        alone(fills_post(ROWS, 0)),
    ]
    for p in range(1, PAIRS):
        fills = [fills_prep(FWD, p - 1)] + ([fills_post(BWD, p - 2)] if p > 1 else [])
        parts.append(item(ROWS, p, *reversed(fills)))
        fills = [fills_post(ROWS, p), fills_prep(BWD, p - 1)]
        if p + 1 < PAIRS:
            fills.append(load(p + 1, 20))
        parts.append(item(FWD, p - 1, *fills))
        parts.append(item(BWD, p - 1, fills_prep(ROWS, p + 1) if p + 1 < PAIRS else fills_prep(FWD, p)))
    parts.append(item(FWD, PAIRS - 1, fills_post(BWD, PAIRS - 2), fills_prep(BWD, PAIRS - 1)))
    parts.append(item(BWD, PAIRS - 1, drain=True))
    parts.append(alone(fills_post(BWD, PAIRS - 1)))
    step = unit = 0
    for part in parts:
        part["step"] = step
        if part["kind"]:
            step += STEPS
        for slot in part["slots"]:
            for n, (name, kind, pair, i) in enumerate(slot):
                takes = name in BANKED and not (name == "xr" and kind == BWD)
                slot[n] = (name, kind, pair, i, unit if takes else None)
                unit += takes
    return parts


def build_program(nc, x, wpack, out):
    f32, bf16 = mybir.dt.float32, mybir.dt.bfloat16
    ALU, ACT = mybir.AluOpType, mybir.ActivationFunctionType
    PARTS = plan()
    ITEMS = [p for p in PARTS if p["kind"]]
    ALL_STEPS = STEPS * len(ITEMS)

    with ExitStack() as ctx:
        sb = lambda name, shape, dt=f32: ctx.enter_context(nc.sbuf_tensor(name, shape, dt))
        ps = lambda name, shape: ctx.enter_context(nc.psum_tensor(name, shape, f32))
        sem = lambda name: ctx.enter_context(nc.semaphore(name))

        wp = sb("wp", [P, NCOL])
        sel = sb("sel", [C, 2, NS], bf16)
        sel_m = sb("sel_m", [C, NS, 2, P // 2], bf16)
        io = sb("io", [C, 2, T])
        x1 = sb("x1", [C, 2, T])
        xr = sb("xr", [P, TILES, T])
        xs = sb("xs", [P, TILES, T])
        th = sb("th", [P, 2, HALF])
        yv = {k: sb(f"yv_{k}", [P, TILES, T]) for k in (ROWS, FWD)}
        sz = {k: sb(f"sz_{k}", [P, TILES, T]) for k in (ROWS, FWD)}
        delta_ab = sb("delta_ab", [P, 2, T])
        u_ab = sb("u_ab", [P, 2, T])
        delta_m = {k: sb(f"delta_{k}", [P, T]) for k in LAYER}
        u_m = {k: sb(f"u_{k}", [P, T]) for k in LAYER}
        b_in = {k: sb(f"b_{k}", [C, T], bf16) for k in LAYER}
        c_in = {k: sb(f"c_{k}", [C, T], bf16) for k in LAYER}
        dbl = sb("dbl", [P, 4, HALF])
        part_hi = sb("part_hi", [C, HALF], bf16)
        part_mid = sb("part_mid", [C, HALF], bf16)
        parts3 = sb("parts3", [C, HALF], bf16)
        ring = sb("ring", [P, RING, T])
        c_ring = sb("c_ring", [P, 2, T])
        a_ring = sb("a_ring", [P, 2, T])
        eps = sb("eps", [C, 1])
        neg_a = sb("neg_a", [P, 2, 2 * NS])
        b_ps, c_ps, y_ps = ps("b_ps", [P, T]), ps("c_ps", [P, T]), ps("y_ps", [P, T])
        bank = ps("bank", [P, 2, HALF])

        def col(name, layer=None):
            at, n = _cols[name, layer]
            return wp[:, at:at + n]

        ident = col("ident")
        small = [col("small", l).rearrange("p (m c) -> p m c", m=2) for l in range(2)]
        other = lambda kind, pair: FWD if kind == ROWS and pair == 0 else kind
        delta_of = lambda kind, pair, k: delta_ab[:, k, :] if k < 2 else delta_m[other(kind, pair)][:, :]
        u_of = lambda kind, pair, k: u_ab[:, k, :] if k < 2 else u_m[other(kind, pair)][:, :]

        def y_name(kind, pair):
            if kind == ROWS:
                return FWD if pair == 0 else ROWS
            return ROWS if pair == PAIRS - 1 else FWD

        yv_of = lambda kind, pair, k: yv[y_name(kind, pair)][:, k, :]
        sz_of = lambda kind, pair, k: sz[y_name(kind, pair)][:, k, :]
        half = lambda ap, j: ap[:, j * HALF:(j + 1) * HALF]
        m_of = lambda k: 0 if k < 2 else 1
        squares = lambda b: xr[0:C, b, :]

        s_sel, s_w, s_const, s_nega = sem("sel_made"), sem("weights_in"), sem("constants_ready"), sem("a_made")
        b_ready, b_used = sem("b_ready"), sem("b_used")
        c_ready, c_copied = sem("c_ready"), sem("c_copied")
        a_ready, h_ready = sem("a_ready"), sem("h_ready")
        g_ready, g_summed, y_taken = sem("g_ready"), sem("g_summed"), sem("y_taken")
        bank_full = [sem(f"bank{i}_full") for i in range(2)]
        bank_free = [sem(f"bank{i}_free") for i in range(2)]
        K = {n: {k: sem(f"{n}_{k}") for k in LAYER} for n in (
            "xr_ready", "conv_done", "tanh_ready", "silu_done", "skip_done", "dbl_ready", "hi_done",
            "mid_ready", "lo_done", "bc_loaded", "dt_ready", "dt_capped", "dt_logged", "dt_done", "u_done", "set_ready")}
        z_tanh = {k: sem(f"z_tanh_{k}") for k in (ROWS, FWD)}
        gate_done = {k: sem(f"gate_done_{k}") for k in (ROWS, FWD)}
        gated_done = {k: sem(f"gated_done_{k}") for k in (ROWS, BWD)}
        x_loaded, wout_done, out_ready, out_stored = sem("x_loaded"), sem("wout_done"), sem("out_ready"), sem("out_stored")
        mean_done, square_done, var_done = sem("mean_done"), sem("square_done"), sem("var_done")
        logged, rstd_done, norm_done, affine_done = sem("logged"), sem("rstd_done"), sem("norm_done"), sem("affine_done")

        block = ctx.enter_context(nc.Block())

        def wait(eng, s, value):
            if value > 0:
                eng.wait_ge(s, value)

        def step_at(g):
            it = ITEMS[g // STEPS]
            s = g % STEPS
            return it["kind"], it["pair"], s // NS, s % NS

        def walk(slot_begin, look_ahead, slot_mid, job, drained):
            for n, part in enumerate(PARTS):
                if not part["kind"]:
                    for j in part["slots"][0]:
                        job(*j)
                    continue
                g0 = part["step"]
                if not PARTS[n - 1]["kind"]:
                    look_ahead(g0)
                for s in range(STEPS):
                    g = g0 + s
                    pending = not (s < 2 and not PARTS[n - 1]["kind"])
                    slot_begin(g, pending)
                    if not (part["drain"] and s == STEPS - 1):
                        look_ahead(g + 1)
                    slot_mid(g)
                    for j in part["slots"][s]:
                        job(*j)
                    drained(g, pending, part["drain"] and s == STEPS - 1)

        nothing = lambda *_: None

        @block.sync
        def _(sp):
            sp.dma_start(wp[:, :], wpack).then_inc(s_w, 16)

            def job(name, kind, pair, i, unit):
                if name == "load":
                    wait(sp, z_tanh[ROWS], 6 * pair)
                    wait(sp, out_stored, 64 * (pair - 2))
                    for b in range(2):
                        sp.dma_start(io[:, b, :], x[2 * pair + b]).then_inc(x_loaded, 16)
                elif name == "bc_in":
                    b, j = i // 2, i % 2
                    k2 = other(kind, pair)
                    wait(sp, K["lo_done"][kind], 4 * pair + i + 1)
                    for dst, at in ((b_in, 0), (c_in, 3 * NS)):
                        sp.dma_start(half(dst[k2][b * 3 * NS:(b + 1) * 3 * NS, :], j),
                                     parts3[at:at + 3 * NS, :]).then_inc(K["bc_loaded"][kind], 16)
                elif name == "w_out" and kind == BWD:
                    b, j = i // 2, i % 2
                    wait(sp, out_ready, 4 * pair + i + 1)
                    sp.dma_start(half(out[2 * pair + b], j), half(io[:, b, :], j)).then_inc(out_stored, 16)

            walk(nothing, nothing, nothing, job, nothing)
            sp.wait_ge(out_stored, 64 * PAIRS)

        @block.tensor
        def _(pe):
            pe.wait_ge(s_w, 16)
            pe.wait_ge(s_const, 1)

            def pick(k, n):
                if k < 2:
                    return sel[:, k, n:n + 1].to_broadcast([C, P])
                return sel_m[:, n, :, :].rearrange("p b c -> p (b c)")

            def look_ahead(g):
                if g >= ALL_STEPS:
                    return
                kind, pair, k, n = step_at(g)
                k2 = other(kind, pair)
                if g % STEPS == 0:
                    pe.wait_ge(K["bc_loaded"][kind], 16 * 8 * (pair + 1))
                wait(pe, b_used, g)
                for j in range(2):
                    last = nc.tensor.matmul(half(b_ps[:, :], j), pick(k, n), half(b_in[k2][:, :], j), start=True, stop=True)
                last.then_inc(b_ready, 1)
                wait(pe, c_copied, g)
                for j in range(2):
                    last = nc.tensor.matmul(half(c_ps[:, :], j), pick(k, n), half(c_in[k2][:, :], j), start=True, stop=True)
                last.then_inc(c_ready, 1)

            def sum_state(g):
                n = g % NS
                pe.wait_ge(g_ready, g + 1)
                for j in range(2):
                    if n == 0:
                        wait(pe, y_taken, 2 * (g // NS - 1) + j + 1)
                    last = nc.tensor.matmul(half(y_ps[:, :], j), ident, half(ring[:, g % RING, :], j),
                                            start=(n == 0), stop=(n == NS - 1))
                last.then_inc(g_summed, 1)

            def drained(g, pending, drain):
                if pending:
                    sum_state(g - 2)
                if drain:
                    sum_state(g - 1)
                    sum_state(g)

            def product(unit, rows, terms):
                wait(pe, bank_free[unit % 2], unit // 2)
                for n, (w, m) in enumerate(terms):
                    last = nc.tensor.matmul(bank[0:rows, unit % 2, :], w, m, start=(n == 0), stop=(n == len(terms) - 1))
                last.then_inc(bank_full[unit % 2], 1)

            def by_batch(name, layer, cols, rows=P):
                w = col(name, layer).rearrange("p (v c) -> p v c", v=3)
                return [w[0:rows, v, :] for v in range(3)]

            def job(name, kind, pair, i, unit):
                layer = LAYER[kind]
                k, j = i // 2, i % 2
                if name in ("xr", "z") and unit is not None:
                    src = io if kind == ROWS else x1
                    if name == "xr" and i == 0:
                        if kind == ROWS:
                            pe.wait_ge(x_loaded, 32 * (pair + 1))
                        else:
                            pe.wait_ge(affine_done, 4 * (pair + 1))
                    w = by_batch("w_xr" if name == "xr" else "w_z", layer, P, C)
                    if k < 2:
                        product(unit, P, [(w[0], half(src[:, k, :], j))])
                    else:
                        product(unit, P, [(w[1 + b], half(src[:, b, :], j)) for b in range(2)])
                elif name == "dbl":
                    if i == 0:
                        pe.wait_ge(K["silu_done"][kind], 6 * (pair + 1))
                    w = by_batch("w_dbl", layer, P)
                    product(unit, P, [(w[0], half(xs[:, k, :], j)), (w[1 + k], half(xs[:, 2, :], j))])
                elif name == "dt":
                    if i in (0, 2):
                        pe.wait_ge(K["hi_done"][kind], 4 * (pair + 1))
                    w = by_batch("w_dt", layer, P)
                    if k < 2:
                        product(unit, P, [(w[0], dbl[:, 2 * k + j, :])])
                    else:
                        product(unit, P, [(w[1 + b], dbl[:, 2 * b + j, :]) for b in range(2)])
                elif name == "w_out":
                    if i == 0:
                        pe.wait_ge(gated_done[kind], 3 * (pair + 1))
                    w = by_batch("w_out", layer, C)
                    product(unit, C, [(w[0], half(yv_of(kind, pair, k), j)), (w[1 + k], half(yv_of(kind, pair, 2), j))])
                elif name == "mean":
                    r, c = i // 4, i % 4
                    if r == 0:
                        pe.wait_ge(wout_done, 4 * pair + c + 1)
                    else:
                        pe.wait_ge(affine_done, 4 * pair + c // 2 + 1)
                    product(unit, C, [(col("mean")[0:C, :], half(x1[:, c // 2, :], c % 2))])
                elif name == "var":
                    c = i % 4
                    pe.wait_ge(square_done, 8 * pair + i + 1)
                    product(unit, C, [(col("mean")[0:C, :], half(squares(c // 2), c % 2))])

            walk(nothing, look_ahead, nothing, job, drained)

        @block.scalar
        def _(act):
            act.wait_ge(s_w, 16)
            for layer in range(2):
                nc.scalar.activation(neg_a[:, layer, :], col("a_log", layer), ACT.Exp).then_inc(s_nega, 1)
            act.wait_ge(s_const, 2)

            def look_ahead(g):
                if g >= ALL_STEPS:
                    return
                kind, pair, k, n = step_at(g)
                if n == 0:
                    act.wait_ge(K["set_ready"][kind], 3 * pair + (1, 3, 2)[k])
                wait(act, h_ready, g - 1)
                nc.scalar.activation(a_ring[:, g % 2, :], delta_of(kind, pair, k), ACT.Exp,
                                     scale=neg_a[:, LAYER[kind], m_of(k) * NS + n:m_of(k) * NS + n + 1]).then_inc(a_ready, 1)
                act.wait_ge(c_ready, g + 1)
                wait(act, g_ready, g - 1)
                nc.scalar.activation(c_ring[:, g % 2, :], c_ps[:, :], ACT.Copy).then_inc(c_copied, 1)

            def full(unit):
                act.wait_ge(bank_full[unit % 2], unit // 2 + 1)
                return bank[:, unit % 2, :]

            def job(name, kind, pair, i, unit):
                layer = LAYER[kind]
                k, j = i // 2, i % 2
                sm = small[layer]
                if name == "xr":
                    src = half(xr[:, k, :], j)
                    if unit is not None:
                        src = full(unit)
                        nc.scalar.activation(half(xr[:, k, :], j), src, ACT.Copy)
                    done = nc.scalar.activation(half(xs[:, k, :], j), src, ACT.Identity,
                                                scale=sm[:, m_of(k), 3:4], bias=sm[:, m_of(k), 4:5])
                    done.then_inc(K["xr_ready"][kind], 1)
                    if unit is not None:
                        act.wait_ge(K["xr_ready"][kind], 6 * pair + i + 1)
                        act.sem_inc(bank_free[unit % 2], 1)
                elif name == "tanh":
                    act.wait_ge(K["conv_done"][kind], 9 * pair + 3 * (k + 1))
                    wait(act, K["silu_done"][kind], 6 * pair + i - 1 if i >= 2 else 0)
                    nc.scalar.activation(th[:, i % 2, :], half(xs[:, k, :], j), ACT.Tanh).then_inc(K["tanh_ready"][kind], 1)
                elif name == "skip" and kind != BWD:
                    act.wait_ge(K["silu_done"][kind], 6 * pair + 2 * (i + 1))
                    nc.scalar.activation(yv_of(kind, pair, i), xs[:, i, :], ACT.Identity,
                                         scale=sm[:, m_of(i), 6:7]).then_inc(K["skip_done"][kind], 1)
                elif name == "z":
                    src = full(unit)
                    if i < 2:
                        act.wait_ge(K["silu_done"][kind], 6 * (pair + 1))
                    else:
                        act.wait_ge(gate_done[kind], 6 * pair + i - 1)
                    nc.scalar.activation(half(sz_of(kind, pair, k), j), src, ACT.Copy)
                    nc.scalar.activation(th[:, i % 2, :], src, ACT.Tanh, scale=0.5).then_inc(z_tanh[kind], 1)
                    act.wait_ge(z_tanh[kind], 6 * pair + i + 1)
                    act.sem_inc(bank_free[unit % 2], 1)
                elif name == "dbl":
                    src = full(unit)
                    wait(act, K["hi_done"][kind], 4 * pair + i if i else 0)
                    nc.scalar.activation(part_hi[:, :], src[0:C, :], ACT.Copy)
                    nc.scalar.activation(dbl[:, i, :], src, ACT.Copy).then_inc(K["dbl_ready"][kind], 1)
                    act.wait_ge(K["dbl_ready"][kind], 4 * pair + i + 1)
                    act.sem_inc(bank_free[unit % 2], 1)
                elif name == "split_mid":
                    act.wait_ge(K["hi_done"][kind], 4 * pair + i + 1)
                    wait(act, K["lo_done"][kind], 4 * pair + i if i else 0)
                    nc.scalar.activation(part_mid[:, :], dbl[0:C, i, :], ACT.Copy).then_inc(K["mid_ready"][kind], 1)
                elif name == "dt":
                    src = full(unit)
                    if k < 2 and pair + (kind != ROWS):
                        act.wait_ge(b_used, scanning[0] + NS * (k + 1))
                    nc.scalar.activation(half(u_of(kind, pair, k), j), src, ACT.Identity, bias=sm[:, m_of(k), 5:6])
                    nc.scalar.activation(half(delta_of(kind, pair, k), j), src, ACT.Exp,
                                         bias=sm[:, m_of(k), 5:6]).then_inc(K["dt_ready"][kind], 1)
                    seen = {0: 1, 1: 2, 4: 3, 5: 4, 2: 5, 3: 6}[i]
                    act.wait_ge(K["dt_ready"][kind], 6 * pair + seen)
                    act.sem_inc(bank_free[unit % 2], 1)
                elif name == "dt_ln":
                    seen = {0: 1, 2: 2, 1: 3}[i]
                    act.wait_ge(K["dt_capped"][kind], 3 * pair + seen)
                    nc.scalar.activation(delta_of(kind, pair, i), delta_of(kind, pair, i), ACT.Ln,
                                         bias=1.0).then_inc(K["dt_logged"][kind], 1)
                elif name == "w_out":
                    src = full(unit)
                    dst = half((x1 if kind == ROWS else io)[:, k, :], j)
                    s, n = (wout_done, 4 * pair + i + 1) if kind == ROWS else (out_ready, 4 * pair + i + 1)
                    nc.scalar.activation(dst, src[0:C, :], ACT.Copy).then_inc(s, 1)
                    act.wait_ge(s, n)
                    act.sem_inc(bank_free[unit % 2], 1)
                elif name == "square":
                    c = i % 4
                    act.wait_ge(mean_done, 8 * pair + i + 1)
                    nc.scalar.activation(half(squares(c // 2), c % 2), half(x1[:, c // 2, :], c % 2),
                                         ACT.Square).then_inc(square_done, 1)
                elif name == "var":
                    c = i % 4
                    src = full(unit)
                    nc.scalar.activation(half(squares(c // 2), c % 2), src[0:C, :], ACT.Copy).then_inc(var_done, 1)
                    act.wait_ge(var_done, 8 * pair + i + 1)
                    act.sem_inc(bank_free[unit % 2], 1)
                elif name == "rstd":
                    nc.scalar.activation(xr[0:C, 0:2, :], xr[0:C, 0:2, :], ACT.Ln, bias=eps[:, :]).then_inc(logged, 1)
                    act.wait_ge(logged, 2 * pair + i + 1)
                    nc.scalar.activation(xr[0:C, 0:2, :], xr[0:C, 0:2, :], ACT.Exp, scale=-0.5).then_inc(rstd_done, 1)
                elif name == "affine":
                    r, b = i // 2, i % 2
                    act.wait_ge(norm_done, 4 * pair + i + 1)
                    ln = col("ln")
                    nc.scalar.activation(x1[:, b, :], x1[:, b, :], ACT.Identity, scale=ln[0:C, 2 * r:2 * r + 1],
                                         bias=ln[0:C, 2 * r + 1:2 * r + 2]).then_inc(affine_done, 1)

            scanning = [0]

            def slot_begin(g, pending):
                scanning[0] = g // STEPS * STEPS

            walk(slot_begin, look_ahead, nothing, job, nothing)

        @block.vector
        def _(dve):
            dve.wait_ge(s_w, 16)
            nc.vector.memset(eps[:, :], EPS)
            nc.vector.tensor_copy(sel[:, :, :], col("sel")[0:C, :].rearrange("p (b n) -> p b n", b=2)).then_inc(s_sel, 1)
            dve.wait_ge(s_sel, 1)
            for b in range(2):
                last = nc.vector.tensor_copy(sel_m[:, :, b, :],
                                             sel[:, b, :].rearrange("p (n o) -> p n o", o=1).to_broadcast([C, NS, P // 2]))
            last.then_inc(s_const, 1)
            dve.wait_ge(s_nega, 2)
            for layer in range(2):
                w = small[layer][:, :, 0:5]
                nc.vector.tensor_scalar(w, w, 0.5, None, ALU.mult)
                wo = col("w_out", layer)
                nc.vector.tensor_scalar(wo, wo, 0.5, None, ALU.mult)
            last = nc.vector.tensor_scalar(neg_a[:, :, :], neg_a[:, :, :], -1.0, None, ALU.mult)
            last.then_inc(s_const, 1)

            def look_ahead(g):
                if g >= ALL_STEPS:
                    return
                kind, pair, k, n = step_at(g)
                if n == 0:
                    dve.wait_ge(K["set_ready"][kind], 3 * pair + (1, 3, 2)[k])
                wait(dve, g_summed, g - RING + 1)
                dve.wait_ge(b_ready, g + 1)
                nc.vector.tensor_tensor(ring[:, g % RING, :], u_of(kind, pair, k), b_ps[:, :], ALU.mult).then_inc(b_used, 1)

            def take(tile):
                it = ITEMS[tile // TILES]
                kind, pair, k = it["kind"], it["pair"], tile % TILES
                dve.wait_ge(K["skip_done"][kind], 3 * pair + k + 1)
                if kind == FWD:
                    dve.wait_ge(K["skip_done"][BWD], 3 * pair + k + 1)
                if kind == BWD:
                    dve.wait_ge(y_taken, 2 * (tile - TILES + 1))
                dve.wait_ge(g_summed, NS * (tile + 1))
                for j in range(2):
                    y = half(yv_of(kind, pair, k), j)
                    nc.vector.tensor_tensor(y, y, half(y_ps[:, :], j), ALU.add).then_inc(y_taken, 1)

            def slot_begin(g, pending):
                if g % NS == 2 and g >= NS and (pending or g % STEPS > 2):
                    if not (g % STEPS == 2 and not follows[g // STEPS]):
                        take(g // NS - 1)

            follows = [PARTS[PARTS.index(it) - 1]["kind"] is not None for it in ITEMS]

            def slot_mid(g):
                kind, pair, k, n = step_at(g)
                dve.wait_ge(a_ready, g + 1)
                dve.wait_ge(b_used, g + 1)
                a, h = a_ring[:, g % 2, :], ring[:, g % RING, :]
                if kind == BWD:
                    a, h = a[:, ::-1], h[:, ::-1]
                nc.vector.tensor_tensor_scan(out=h, data0=a, data1=h, initial=0.0,
                                             op0=ALU.mult, op1=ALU.add).then_inc(h_ready, 1)

            def drained(g, pending, drain):
                if drain:
                    take(g // NS)

            def job(name, kind, pair, i, unit):
                layer = LAYER[kind]
                k, j = i // 2, i % 2
                sm = small[layer]
                if name == "conv":
                    k, m = i // 3, i % 3
                    d = TAPS - 1 - m
                    if m == 0:
                        dve.wait_ge(K["xr_ready"][kind], 6 * pair + 2 * (k + 1))
                    wait(dve, K["conv_done"][kind], 9 * pair + i if m else 0)
                    acc, src = xs[:, k, :], xr[:, k, :]
                    if kind == ROWS:
                        acc = acc.rearrange("p (s t) -> p s t", t=W)[:, :, d:W]
                        src = src.rearrange("p (s t) -> p s t", t=W)[:, :, 0:W - d]
                    elif kind == FWD:
                        acc, src = acc[:, d:T], src[:, 0:T - d]
                    else:
                        acc, src = acc[:, 0:T - d], src[:, d:T]
                    nc.vector.scalar_tensor_tensor(out=acc, in0=src, scalar=sm[:, m_of(k), m:m + 1], in1=acc,
                                                   op0=ALU.mult, op1=ALU.add).then_inc(K["conv_done"][kind], 1)
                elif name == "silu":
                    dve.wait_ge(K["tanh_ready"][kind], 6 * pair + i + 1)
                    v = half(xs[:, k, :], j)
                    nc.vector.scalar_tensor_tensor(out=v, in0=th[:, i % 2, :], scalar=1.0, in1=v,
                                                   op0=ALU.add, op1=ALU.mult).then_inc(K["silu_done"][kind], 1)
                elif name == "skip" and kind == BWD:
                    dve.wait_ge(K["skip_done"][FWD], 3 * pair + i + 1)
                    dve.wait_ge(K["silu_done"][kind], 6 * pair + 2 * (i + 1))
                    y = yv_of(kind, pair, i)
                    nc.vector.scalar_tensor_tensor(out=y, in0=xs[:, i, :], scalar=sm[:, m_of(i), 6:7], in1=y,
                                                   op0=ALU.mult, op1=ALU.add).then_inc(K["skip_done"][kind], 1)
                elif name == "gate":
                    dve.wait_ge(z_tanh[kind], 6 * pair + i + 1)
                    v = half(sz_of(kind, pair, k), j)
                    nc.vector.scalar_tensor_tensor(out=v, in0=th[:, i % 2, :], scalar=1.0, in1=v,
                                                   op0=ALU.add, op1=ALU.mult).then_inc(gate_done[kind], 1)
                elif name == "split_hi":
                    dve.wait_ge(K["dbl_ready"][kind], 4 * pair + i + 1)
                    v = dbl[0:C, i, :]
                    nc.vector.scalar_tensor_tensor(out=v, in0=part_hi[:, :], scalar=col("split")[0:C, 0:1], in1=v,
                                                   op0=ALU.mult, op1=ALU.add).then_inc(K["hi_done"][kind], 1)
                elif name == "split_lo":
                    dve.wait_ge(K["mid_ready"][kind], 4 * pair + i + 1)
                    loaded = 16 * 2 * (4 * pair + i)
                    wait(dve, K["bc_loaded"][kind], loaded if i else 0)
                    nc.vector.scalar_tensor_tensor(out=parts3[:, :], in0=part_mid[:, :],
                                                   scalar=col("split")[0:C, 1:2], in1=dbl[0:C, i, :],
                                                   op0=ALU.mult, op1=ALU.add).then_inc(K["lo_done"][kind], 1)
                elif name == "dt_max":
                    seen = {0: 1, 2: 2, 1: 3}[i]
                    dve.wait_ge(K["dt_logged"][kind], 3 * pair + seen)
                    d = delta_of(kind, pair, i)
                    nc.vector.tensor_tensor(d, d, u_of(kind, pair, i), ALU.max).then_inc(K["dt_done"][kind], 1)
                elif name == "mean":
                    c = i % 4
                    dve.wait_ge(bank_full[unit % 2], unit // 2 + 1)
                    v = half(x1[:, c // 2, :], c % 2)
                    nc.vector.tensor_tensor(v, v, bank[0:C, unit % 2, :], ALU.subtract).then_inc(mean_done, 1)
                    dve.wait_ge(mean_done, 8 * pair + i + 1)
                    dve.sem_inc(bank_free[unit % 2], 1)

            walk(slot_begin, look_ahead, slot_mid, job, drained)

        @block.gpsimd
        def _(pool):
            def slot_mid(g):
                pool.wait_ge(h_ready, g + 1)
                pool.wait_ge(c_copied, g + 1)
                r = ring[:, g % RING, :]
                nc.gpsimd.tensor_tensor(r, r, c_ring[:, g % 2, :], ALU.mult).then_inc(g_ready, 1)

            def job(name, kind, pair, i, unit):
                if name == "dt_cap":
                    seen = {0: 2, 2: 4, 1: 6}[i]
                    pool.wait_ge(K["dt_ready"][kind], 6 * pair + seen)
                    d = delta_of(kind, pair, i)
                    nc.gpsimd.tensor_scalar(d, d, LN_CAP, 0.0, ALU.min, ALU.max).then_inc(K["dt_capped"][kind], 1)
                elif name == "u":
                    seen = {0: 1, 2: 2, 1: 3}[i]
                    pool.wait_ge(K["dt_done"][kind], 3 * pair + seen)
                    d = delta_of(kind, pair, i)
                    nc.gpsimd.tensor_tensor(u_of(kind, pair, i), d, xs[:, i, :], ALU.mult).then_inc(K["u_done"][kind], 1)
                    pool.wait_ge(K["u_done"][kind], 3 * pair + seen)
                    if kind == ROWS:
                        starts = d.rearrange("p (s t) -> p s t", t=W)[:, :, 0:1]
                        nc.gpsimd.memset(starts, BIG).then_inc(K["set_ready"][kind], 1)
                    else:
                        pool.sem_inc(K["set_ready"][kind], 1)
                elif name == "gated":
                    pool.wait_ge(y_taken, 2 * (tile_of(kind, pair) + i + 1))
                    pool.wait_ge(gate_done[ROWS if kind == ROWS else FWD], 6 * (pair + 1))
                    y = yv_of(kind, pair, i)
                    nc.gpsimd.tensor_tensor(y, y, sz_of(kind, pair, i), ALU.mult).then_inc(gated_done[kind], 1)
                elif name == "norm":
                    r, b = i // 2, i % 2
                    pool.wait_ge(rstd_done, 2 * pair + r + 1)
                    nc.gpsimd.tensor_tensor(x1[:, b, :], x1[:, b, :], squares(b), ALU.mult).then_inc(norm_done, 1)

            def tile_of(kind, pair):
                n = next(n for n, it in enumerate(ITEMS) if it["kind"] == kind and it["pair"] == pair)
                return TILES * n

            walk(nothing, nothing, slot_mid, job, nothing)


def pack(inputs):
    wp = np.zeros((P, NCOL), np.float32)

    def put(name, layer, a, row=0, at=0):
        c = _cols[name, layer][0] + at
        wp[row:row + a.shape[0], c:c + a.shape[1]] = a

    for layer, pre in enumerate(("L0_conv_", "L1_conv_")):
        g = lambda n: np.asarray(inputs[pre + n])
        w_in, w_x, w_dt, w_out = g("W_in"), g("W_x" if layer == 0 else "W_xproj"), g("W_dt"), g("W_out")
        for name, w in (("w_xr", w_in[:, :DI]), ("w_z", w_in[:, DI:])):
            put(name, layer, w[:, :P])
            put(name, layer, w[:, P:], 0, P)
            put(name, layer, w[:, P:], 0, 2 * P + DM)
        bb, cc, dt = w_x[:, RANK:RANK + NS], w_x[:, RANK + NS:], w_x[:, :RANK]
        w = np.concatenate([bb] * 3 + [cc] * 3 + [dt], axis=1)
        put("w_dbl", layer, w[:P])
        put("w_dbl", layer, w[P:], 0, P)
        put("w_dbl", layer, w[P:], DM, 2 * P)
        put("w_dt", layer, w_dt[:, :P], 6 * NS)
        put("w_dt", layer, w_dt[:, P:], 6 * NS, P)
        put("w_dt", layer, w_dt[:, P:], 6 * NS, 2 * P + DM)
        put("w_out", layer, w_out[:P])
        put("w_out", layer, w_out[P:], 0, C)
        put("w_out", layer, w_out[P:], DM, 2 * C)
        rows = np.concatenate([g("conv_w").reshape(DI, TAPS), g("conv_b")[:, None], g("b_dt")[:, None], g("D")[:, None]], axis=1)
        for name, a in (("small", rows), ("a_log", g("A_log"))):
            put(name, layer, a[:P])
            put(name, layer, a[P:], 0, a.shape[1])
            put(name, layer, a[P:], DM, a.shape[1])
        put("ln", None, np.stack([g("ln_g"), g("ln_b")], axis=1), 0, 2 * layer)
    put("ident", None, np.eye(P, dtype=np.float32))
    put("mean", None, np.full((C, C), 1.0 / C, np.float32))
    sel = np.zeros((C, 2, NS), np.float32)
    split = np.zeros((C, 2), np.float32)
    for b in range(2):
        for g in range(3):
            for n in range(NS):
                sel[(b * 3 + g) * NS + n, b, n] = 1.0
                split[(b * 3 + g) * NS + n] = (-1.0 if g >= 1 else 0.0, -1.0 if g == 2 else 0.0)
    put("sel", None, sel.reshape(C, 2 * NS))
    put("split", None, split)
    return wp


def kernel(**inputs):
    import concourse.bacc as bacc
    from concourse.bass_utils import run_bass_kernel_spmd

    nc = bacc.Bacc("TRN2", target_bir_lowering=False, num_devices=1)
    arrays = {"x": np.ascontiguousarray(np.asarray(inputs["x"]).reshape(B, C, T)), "wpack": pack(inputs)}
    x = nc.dram_tensor("x", (B, C, T), mybir.dt.float32, kind="ExternalInput").ap()
    wpack = nc.dram_tensor("wpack", (P, NCOL), mybir.dt.float32, kind="ExternalInput").ap()
    out = nc.dram_tensor("out", (B, C, T), mybir.dt.float32, kind="ExternalOutput").ap()
    build_program(nc, x, wpack, out)
    r = run_bass_kernel_spmd(nc, [arrays], core_ids=[0])
    return r.results[0]["out"].reshape(B, C, H, W)
```

```python
import numpy as np
import concourse.bass as bass
from concourse import mybir
from contextlib import ExitStack

B, C, H, W = 8, 96, 32, 32
T = H * W
DI = 2 * C
NS = 16
RANK = C // 16
TAPS = 4
P = 128
DM = DI - P
PAIRS = B // 2
HALF = T // 2
BIG = 1.0e34
EPS = 1e-5

ROWS, FWD, BWD = "rows", "fwd", "bwd"
LAYER = {ROWS: 0, FWD: 1, BWD: 1}
TILES = 3
BC_ROWS = 4 * NS
X_ROWS = BC_ROWS + 2 * RANK
DT_TERMS = ((0, 0), (0, 1), (1, 0), (1, 1), (0, 2), (2, 0))
DT_ROWS = 2 * RANK * len(DT_TERMS)
STEPS = TILES * NS
RING = 5
C_RING = 4
A_RING = 2

_cols, _at = {}, 0
for _name, _n in [("w_xr", 3 * P), ("w_z", 3 * P), ("w_dbl", 3 * X_ROWS), ("w_out", 3 * C),
                  ("small", 2 * 7), ("a_log", 2 * NS)]:
    for _layer in range(2):
        _cols[_name, _layer] = (_at, _n)
        _at += _n
for _name, _n in [("ident", P), ("mean", C), ("centre", C), ("sel", 2 * NS), ("split", 2), ("ln", 4)]:
    _cols[_name, None] = (_at, _n)
    _at += _n
NKEPT = _at
for _layer in range(2):
    _cols["w_dt", _layer] = (_at, 3 * P)
    _at += 3 * P
NCOL = _at


PE_ORDER = ("ahead", "jobs", "sum")
DVE_ORDER = ("scan", "take", "ahead", "jobs", "last")
SUM_LAG = 2


def fills_prep(kind, pair):
    out = []
    for u in range(6):
        out.append((PREP["xr"][u], "xr", u))
    for k in range(TILES):
        for m in range(TAPS - 1):
            out.append((PREP["conv"][k] + m, "conv", 3 * k + m))
        for j in range(2):
            out.append((PREP["tanh"][k] + j, "tanh", 2 * k + j))
            out.append((PREP["tanh"][k] + 1 + j, "silu", 2 * k + j))
        out.append((PREP["skip"][k], "skip", k))
    for j in range(2):
        for n, name in enumerate(("dbl", "split_hi", "split_mid", "split_lo", "bc_in")):
            out.append((PREP["dbl"][j] + n, name, j))
    for u in range(6):
        out.append((PREP["dt"][u], "dt", u))
    for k in range(TILES):
        out.append((PREP["ln"][k], "dt_ln", k))
        out.append((PREP["u"][k], "u", k))
    if kind != BWD:
        for u in range(6):
            out.append((PREP["z"][u], "z", u))
            out.append((PREP["z"][u] + 1, "gate", u))
    return [(s, name, kind, pair, i) for s, name, i in sorted(out, key=lambda x: x[0])]


def fills_post(kind, pair):
    t = POST[kind]
    out = [(t["gated"][k], "gated", k) for k in range(TILES)]
    out += [(t["w_out"][c], "w_out", c) for c in range(4)]
    if kind == ROWS:
        out += [(t["centre"][c], "centre", c) for c in range(4)]
        out += [(t["var"][c], "var", c) for c in range(8)]
        out += [(t["rstd"][r], "rstd", r) for r in range(2)]
        out += [(t["norm"][i], "norm", i) for i in range(4)]
        out += [(t["affine"][i], "affine", i) for i in range(2)]
    return [(s, name, kind, pair, i) for s, name, i in sorted(out, key=lambda x: x[0])]


PREP = dict(xr=(0, 2, 2, 3, 4, 5), conv=(2, 4, 6), tanh=(5, 7, 9), skip=(12, 13, 14), dbl=(12, 14), dt=(21, 22, 33, 34, 21, 24), ln=(25, 37, 27), u=(26, 39, 28), z=(36, 36, 38, 39, 40, 41))
POST = {ROWS: dict(gated=(2, 4, 6), w_out=(9, 10, 11, 12), var=(14, 15, 16, 17, 33, 34, 35, 36), rstd=(23, 39), norm=(26, 28, 40, 42), centre=(28, 29, 30, 31), affine=(45, 47)),
        BWD: dict(gated=(0, 1, 4), w_out=(6, 7, 8, 9))}
LATER = {"skip": (0, 1, 2), "dt": {4: 1, 5: 2, 2: 6, 3: 7}, "dt_ln": {2: 3, 1: 9}, "u": {2: 4, 1: 10}}
FAST_POST = dict(gated=(0, 1, 3), w_out=(4, 5, 6, 7), var=(6, 7, 8, 9, 19, 20, 21, 22), rstd=(11, 24),
                 norm=(13, 14, 26, 27), centre=(16, 16, 18, 18), affine=(28, 29))


BANKED = {"xr", "z", "dbl", "dt", "w_out", "centre", "var"}


def plan():
    def item(kind, pair, *fills):
        slots = [[] for _ in range(STEPS)]
        for f in fills:
            for s, *job in f:
                slots[s].append(tuple(job))
        return {"kind": kind, "pair": pair, "slots": slots}

    def alone(*fills):
        jobs = sorted((x for f in fills for x in f), key=lambda x: x[0])
        return {"kind": None, "slots": [[tuple(x[1:]) for x in jobs]]}

    load = lambda pair, slot: [(slot, "load", ROWS, pair, 0)]
    now, later = load(0, -2) + load(1, -1), []
    for s, name, kind, pair, i in fills_prep(ROWS, 0):
        if name in ("z", "gate"):
            later.append((2 * i + 12 + (name == "gate"), name, kind, pair, i))
        elif name == "skip":
            later.append((LATER[name][i], name, kind, pair, i))
        elif name in LATER and i in LATER[name]:
            later.append((LATER[name][i], name, kind, pair, i))
        else:
            now.append((s, name, kind, pair, i))
    later.sort(key=lambda x: x[0])
    second = [(11 + s * 34 // 44, *r) for s, *r in fills_prep(ROWS, 1)]
    usual = dict(POST[ROWS])
    POST[ROWS].update(FAST_POST)
    first_post = fills_post(ROWS, 0)
    POST[ROWS].update(usual)
    start = 30
    fwd = [(s + start, *r) for s, *r in fills_prep(FWD, 0) if r[0] not in ("z", "gate")]
    first_z = [(i + (name == "gate"), name, kind, pair, i) for s, name, kind, pair, i in fills_prep(FWD, 0)
               if name in ("z", "gate")]
    parts = [
        alone(now),
        item(ROWS, 0, later, second),
        item(ROWS, 1, first_post, [x for x in fwd if x[0] < STEPS and x[1] not in ("dt", "dt_ln", "u")]),
        alone([x for x in fwd if x[0] >= STEPS or x[1] in ("dt", "dt_ln", "u")]),
    ]
    for p in range(1, PAIRS):
        if p > 1:
            parts.append(item(ROWS, p, fills_post(BWD, p - 2), fills_prep(FWD, p - 1)))
        fills = [fills_post(ROWS, p), fills_prep(BWD, p - 1)]
        if p == 1:
            fills.insert(0, first_z)
        if p + 1 < PAIRS:
            fills.append(load(p + 1, 20))
        parts.append(item(FWD, p - 1, *fills))
        parts.append(item(BWD, p - 1, fills_prep(ROWS, p + 1) if p + 1 < PAIRS else fills_prep(FWD, p)))
    parts.append(item(FWD, PAIRS - 1, fills_post(BWD, PAIRS - 2), fills_prep(BWD, PAIRS - 1)))
    parts.append(item(BWD, PAIRS - 1))
    parts.append(alone(fills_post(BWD, PAIRS - 1)))
    step = unit = use = 0
    for part in parts:
        part["step"] = step
        if part["kind"]:
            step += STEPS
        for slot in part["slots"]:
            for n, (name, kind, pair, i) in enumerate(slot):
                takes = name in BANKED and not (name == "xr" and kind == BWD)
                tanh = name in ("tanh", "z")
                slot[n] = (name, kind, pair, i, unit if takes else None, use if tanh else None)
                unit += takes
                use += tanh
    return parts


def build_program(nc, x, wpack, out):
    f32, bf16 = mybir.dt.float32, mybir.dt.bfloat16
    ALU, ACT = mybir.AluOpType, mybir.ActivationFunctionType
    PARTS = plan()
    ITEMS = [p for p in PARTS if p["kind"]]
    ALL_STEPS = STEPS * len(ITEMS)

    with ExitStack() as ctx:
        sb = lambda name, shape, dt=f32: ctx.enter_context(nc.sbuf_tensor(name, shape, dt))
        ps = lambda name, shape: ctx.enter_context(nc.psum_tensor(name, shape, f32))
        sem = lambda name: ctx.enter_context(nc.semaphore(name))

        wp = sb("wp", [P, NKEPT])
        sel = sb("sel", [C, 2, NS], bf16)
        sel_m = sb("sel_m", [C, NS, 2, P // 2], bf16)
        io = sb("io", [C, 2, T])
        x1 = sb("x1", [C, 2, T])
        xr = sb("xr", [P, TILES, T])
        xs = sb("xs", [P, TILES, T])
        th = sb("th", [P, 2, HALF])
        yv = {k: sb(f"yv_{k}", [P, TILES, T]) for k in (ROWS, FWD)}
        sz = {k: sb(f"sz_{k}", [P, TILES, T]) for k in (ROWS, FWD)}
        delta_ab = sb("delta_ab", [P, 2, T])
        u_ab = sb("u_ab", [P, 2, T])
        delta_m = sb("delta_m", [P, 2, T])
        u_m = sb("u_m", [P, 2, T])
        b_in = sb("b_in", [C, 2, T], bf16)
        c_in = sb("c_in", [C, 2, T], bf16)
        dbl = sb("dbl", [X_ROWS, 2, HALF])
        parts3 = sb("parts3", [X_ROWS, 2, 3, HALF], bf16)
        dt_in = sb("dt_in", [DT_ROWS, T], bf16)
        w_dt = sb("w_dt_parts", [DT_ROWS, 2, 3, P], bf16)
        w_centre = sb("w_centre", [C, C])
        b_centre = sb("b_centre", [C, 1])
        w_sum = sb("w_sum", [P, 3])
        ring = sb("ring", [P, RING, T])
        c_ring = sb("c_ring", [P, C_RING, T])
        a_ring = sb("a_ring", [P, A_RING, T])
        eps = sb("eps", [C, 1])
        neg_a = sb("neg_a", [P, 2, 2 * NS])
        b_ps, c_ps, y_ps = ps("b_ps", [P, T]), ps("c_ps", [P, T]), ps("y_ps", [P, T])
        bank = ps("bank", [P, 2, HALF])

        def col(name, layer=None):
            at, n = _cols[name, layer]
            return wp[:, at:at + n]

        ident = col("ident")
        small = [col("small", l).rearrange("p (m c) -> p m c", m=2) for l in range(2)]
        ordinal = {(it["kind"], it["pair"]): n for n, it in enumerate(ITEMS)}
        parity = lambda kind, pair: ordinal[kind, pair] % 2
        delta_of = lambda kind, pair, k: delta_ab[:, k, :] if k < 2 else delta_m[:, parity(kind, pair), :]
        u_of = lambda kind, pair, k: u_ab[:, k, :] if k < 2 else u_m[:, parity(kind, pair), :]

        def y_name(kind, pair):
            if kind == ROWS:
                return FWD if pair == 0 else ROWS
            return ROWS if pair == PAIRS - 1 else FWD

        yv_of = lambda kind, pair, k: yv[y_name(kind, pair)][:, k, :]
        sz_of = lambda kind, pair, k: sz[y_name(kind, pair)][:, k, :]
        half = lambda ap, j: ap[:, j * HALF:(j + 1) * HALF]
        m_of = lambda k: 0 if k < 2 else 1
        squares = lambda b: xr[0:C, b, :]

        s_sel, s_w, s_const, s_nega = sem("sel_made"), sem("weights_in"), sem("constants_ready"), sem("a_made")
        b_ready, b_used = sem("b_ready"), sem("b_used")
        c_ready, c_copied = sem("c_ready"), sem("c_copied")
        a_ready, h_ready = sem("a_ready"), sem("h_ready")
        g_ready, g_summed, y_taken = sem("g_ready"), sem("g_summed"), sem("y_taken")
        produced, evacuated = sem("bank_produced"), sem("bank_evacuated")
        K = {n: {k: sem(f"{n}_{k}") for k in LAYER} for n in (
            "conv_done", "skip_done", "hi_done", "mid_ready", "lo_done", "bc_loaded",
            "dt_exp", "dt_logged", "dt_added", "set_ready")}
        xr_ready, u_done = sem("xr_ready_bwd"), sem("u_done_rows")
        th_ready, th_used = sem("tanh_ready"), sem("tanh_used")
        gated_done = {k: sem(f"gated_done_{k}") for k in (ROWS, BWD)}
        x_loaded = [sem(f"x_loaded_{i}") for i in range(2)]
        out_stored, logged, rstd_done, norm_done = sem("out_stored"), sem("logged"), sem("rstd_done"), sem("norm_done")
        affine_done, s_split, s_centre, s_sums = sem("affine_done"), sem("w_dt_split"), sem("centre_made"), sem("w_sums")

        unit_of = {j[:4]: j[4] for p in PARTS for slot in p["slots"] for j in slot}

        use_of = {j[:4]: j[5] for p in PARTS for slot in p["slots"] for j in slot}
        made = {"silu": "tanh", "gate": "z"}
        order = [use_of[made[j[0]], j[1], j[2], j[3]] for p in PARTS for slot in p["slots"] for j in slot if j[0] in made]
        assert order == sorted(order)

        def halved(eng, name, kind, pair, i):
            eng.wait_ge(th_used, use_of[made[name], kind, pair, i] + 1)

        def landed(eng, name, kind, pair, i):
            eng.wait_ge(evacuated, unit_of[name, kind, pair, i] + 1)

        ready_order = {k: sorted(range(TILES), key=lambda t: (PREP["u"][t], t)) for k in LAYER}
        nth = lambda k: ready_order[ROWS].index(k) + 1

        def source(kind, pair):
            return x1 if kind != ROWS or pair == 1 else io

        LOADS = 16 * 2 * (6 + len(DT_TERMS))

        block = ctx.enter_context(nc.Block())

        def wait(eng, s, value):
            if value > 0:
                eng.wait_ge(s, value)

        def step_at(g):
            it = ITEMS[g // STEPS]
            s = g % STEPS
            return it["kind"], it["pair"], s // NS, s % NS

        def walk(order, job, **phases):
            for n, part in enumerate(PARTS):
                if not part["kind"]:
                    for j in part["slots"][0]:
                        job(*j)
                    continue
                g0 = part["step"]
                if n and not PARTS[n - 1]["kind"] and "ahead" in phases:
                    phases["ahead"](g0)
                for s in range(STEPS):
                    for phase in order:
                        if phase == "jobs":
                            for j in part["slots"][s]:
                                job(*j)
                        elif phase == "ahead":
                            if s < STEPS - 1 or PARTS[n + 1]["kind"]:
                                phases["ahead"](g0 + s + 1)
                        else:
                            phases[phase](g0 + s)

        @block.sync
        def _(sp):
            sp.dma_start(wp[:, :], wpack[:, 0:NKEPT]).then_inc(s_w, 16)
            sp.dma_start(ring[0:DT_ROWS, 0:2, 0:3 * P],
                         wpack[0:DT_ROWS, NKEPT:].rearrange("p (l c) -> p l c", l=2)).then_inc(s_w, 16)

            def job(name, kind, pair, i, unit, use):
                if name == "load":
                    dst = source(kind, pair)
                    if pair > 1:
                        if pair > 2:
                            landed(sp, "z", ROWS, pair - 1, 5)
                        wait(sp, out_stored, 64 * (pair - 2))
                    for b in range(2):
                        sp.dma_start(dst[:, b, :], x[2 * pair + b]).then_inc(x_loaded[pair % 2], 16)
                elif name == "bc_in":
                    cols = slice(i * HALF, (i + 1) * HALF)
                    rows = 2 * NS
                    wait(sp, K["lo_done"][kind], 2 * pair + i + 1)
                    for g in range(3):
                        for dst, at in ((b_in, 0), (c_in, rows)):
                            sp.dma_start(dst[rows * g:rows * (g + 1), parity(kind, pair), cols],
                                         parts3[at:at + rows, i, g, :]).then_inc(K["bc_loaded"][kind], 16)
                    for q, (g, _) in enumerate(DT_TERMS):
                        sp.dma_start(dt_in[2 * RANK * q:2 * RANK * (q + 1), cols],
                                     parts3[BC_ROWS:X_ROWS, i, g, :]).then_inc(K["bc_loaded"][kind], 16)
                elif name == "w_out" and kind == BWD:
                    b, j = i // 2, i % 2
                    landed(sp, name, kind, pair, i)
                    sp.dma_start(half(out[2 * pair + b], j), half(io[:, b, :], j)).then_inc(out_stored, 16)

            walk(("jobs",), job)
            sp.wait_ge(out_stored, 64 * PAIRS)

        @block.tensor
        def _(pe):
            pe.wait_ge(s_w, 32)
            pe.wait_ge(s_const, 1)
            pe.wait_ge(s_split, 8)
            nc.tensor.matmul(bank[0:C, 0, 0:1], col("centre")[0:C, :], col("ln")[0:C, 1:2], start=True, stop=True).then_inc(s_centre, 1)
            pe.wait_ge(s_centre, 2)

            def pick(k, n):
                if k < 2:
                    return sel[:, k, n:n + 1].to_broadcast([C, P])
                return sel_m[:, n, :, :].rearrange("p b c -> p (b c)")

            def look_ahead(g):
                if g >= ALL_STEPS:
                    return
                kind, pair, k, n = step_at(g)
                if g % STEPS == 0:
                    pe.wait_ge(K["bc_loaded"][kind], LOADS * (pair + 1))
                wait(pe, b_used, g)
                for j in range(2):
                    last = nc.tensor.matmul(half(b_ps[:, :], j), pick(k, n), half(b_in[:, parity(kind, pair), :], j), start=True, stop=True)
                last.then_inc(b_ready, 1)
                wait(pe, c_copied, g)
                for j in range(2):
                    last = nc.tensor.matmul(half(c_ps[:, :], j), pick(k, n), half(c_in[:, parity(kind, pair), :], j), start=True, stop=True)
                last.then_inc(c_ready, 1)

            def sum_state(g):
                n = g % NS
                pe.wait_ge(g_ready, g + 1)
                for j in range(2):
                    if n == 0:
                        wait(pe, y_taken, 2 * (g // NS - 1) + j + 1)
                    last = nc.tensor.matmul(half(y_ps[:, :], j), ident, half(ring[:, g % RING, :], j),
                                            start=(n == 0), stop=(n == NS - 1))
                last.then_inc(g_summed, 1)

            def slot_end(g):
                for done in range(g - SUM_LAG, g + 1 if g == ALL_STEPS - 1 else g - SUM_LAG + 1):
                    if done >= 0:
                        sum_state(done)

            def product(unit, rows, terms):
                wait(pe, evacuated, unit - 1)
                for n, (w, m) in enumerate(terms):
                    last = nc.tensor.matmul(bank[0:rows, unit % 2, :], w, m, start=(n == 0), stop=(n == len(terms) - 1))
                last.then_inc(produced, 1)

            def by_batch(name, layer, rows=P):
                w = col(name, layer).rearrange("p (v c) -> p v c", v=3)
                return [w[0:rows, v, :] for v in range(3)]

            def job(name, kind, pair, i, unit, use):
                layer = LAYER[kind]
                k, j = i // 2, i % 2
                if name in ("xr", "z") and unit is not None:
                    src = source(kind, pair)
                    if name == "xr" and i == 0:
                        if kind == ROWS:
                            pe.wait_ge(x_loaded[pair % 2], 32 * (pair // 2 + 1))
                        else:
                            pe.wait_ge(affine_done, 2 * (pair + 1))
                    w = by_batch("w_xr" if name == "xr" else "w_z", layer, C)
                    if k < 2:
                        product(unit, P, [(w[0], half(src[:, k, :], j))])
                    else:
                        product(unit, P, [(w[1 + b], half(src[:, b, :], j)) for b in range(2)])
                elif name == "dbl":
                    halved(pe, "silu", kind, pair, 5)
                    w = by_batch("w_dbl", layer)
                    product(unit, X_ROWS, [(w[k], half(xs[:, k, :], i)) for k in range(TILES)])
                elif name == "dt":
                    pe.wait_ge(K["bc_loaded"][kind], LOADS * (pair + 1))
                    product(unit, P, [(w_dt[:, layer, k, :], half(dt_in[:, :], j))])
                elif name == "w_out":
                    pe.wait_ge(gated_done[kind], 3 * (pair + 1))
                    w = by_batch("w_out", layer)
                    product(unit, C, [(w[0], half(yv_of(kind, pair, k), j)), (w[1 + k], half(yv_of(kind, pair, 2), j))])
                elif name == "centre":
                    pe.wait_ge(norm_done, 4 * pair + k + 1)
                    product(unit, C, [(w_centre[:, :], half(x1[:, k, :], j))])
                elif name == "var":
                    c = i % 4
                    landed(pe, "w_out" if i < 4 else "centre", kind, pair, c)
                    product(unit, C, [(col("mean")[0:C, :], half(squares(c // 2), c % 2))])

            walk(PE_ORDER, job, ahead=look_ahead, sum=slot_end)

        @block.scalar
        def _(act):
            act.wait_ge(s_w, 32)
            for layer in range(2):
                nc.scalar.activation(neg_a[:, layer, :], col("a_log", layer), ACT.Exp).then_inc(s_nega, 1)
            act.wait_ge(s_const, 2)

            def look_ahead(g):
                if g >= ALL_STEPS:
                    return
                kind, pair, k, n = step_at(g)
                if n == 0:
                    act.wait_ge(K["set_ready"][kind], 3 * pair + nth(k))
                wait(act, h_ready, g - A_RING + 1)
                nc.scalar.activation(a_ring[:, g % A_RING, :], delta_of(kind, pair, k), ACT.Exp,
                                     scale=neg_a[:, LAYER[kind], m_of(k) * NS + n:m_of(k) * NS + n + 1]).then_inc(a_ready, 1)
                act.wait_ge(c_ready, g + 1)
                wait(act, g_ready, g - C_RING + 1)
                nc.scalar.activation(c_ring[:, g % C_RING, :], c_ps[:, :], ACT.Copy).then_inc(c_copied, 1)

            def full(unit):
                act.wait_ge(produced, unit + 1)
                return bank[:, unit % 2, :]

            def tanh(src, use, **kw):
                wait(act, th_used, use - 1)
                return nc.scalar.activation(th[:, use % 2, :], src, ACT.Tanh, **kw).then_inc(th_ready, 1)

            def job(name, kind, pair, i, unit, use):
                layer = LAYER[kind]
                k, j = i // 2, i % 2
                sm = small[layer]
                if name == "xr":
                    src = half(xr[:, k, :], j)
                    if ordinal[kind, pair] and j == 0:
                        before = ITEMS[ordinal[kind, pair] - 1]
                        act.wait_ge(K["set_ready"][before["kind"]], 3 * before["pair"] + nth(k))
                    if unit is not None:
                        src = full(unit)
                        nc.scalar.activation(half(xr[:, k, :], j), src, ACT.Copy)
                    nc.scalar.activation(half(xs[:, k, :], j), src, ACT.Identity, scale=sm[:, m_of(k), 3:4],
                                         bias=sm[:, m_of(k), 4:5]).then_inc(xr_ready if unit is None else evacuated, 1)
                elif name == "tanh":
                    act.wait_ge(K["conv_done"][kind], 9 * pair + 3 * (k + 1))
                    tanh(half(xs[:, k, :], j), use)
                elif name == "skip" and kind != BWD:
                    halved(act, "silu", kind, pair, 2 * i + 1)
                    nc.scalar.activation(yv_of(kind, pair, i), xs[:, i, :], ACT.Identity,
                                         scale=sm[:, m_of(i), 6:7]).then_inc(K["skip_done"][kind], 1)
                elif name == "z":
                    src = full(unit)
                    tanh(src, use, scale=0.5)
                    nc.scalar.activation(half(sz_of(kind, pair, k), j), src, ACT.Copy).then_inc(evacuated, 1)
                elif name == "dbl":
                    src = full(unit)[0:X_ROWS, :]
                    nc.scalar.activation(parts3[:, i, 0, :], src, ACT.Copy)
                    nc.scalar.activation(dbl[:, i, :], src, ACT.Copy).then_inc(evacuated, 1)
                elif name == "split_mid":
                    act.wait_ge(K["hi_done"][kind], 2 * pair + i + 1)
                    nc.scalar.activation(parts3[:, i, 1, :], dbl[:, i, :], ACT.Copy).then_inc(K["mid_ready"][kind], 1)
                elif name == "dt":
                    src = full(unit)
                    if k < 2:
                        wait(act, b_used, STEPS * (ordinal[kind, pair] - 1) + NS * (k + 1))
                    bias = sm[:, m_of(k), 5:6]
                    nc.scalar.activation(half(u_of(kind, pair, k), j), src, ACT.Relu, bias=bias)
                    nc.scalar.activation(half(delta_of(kind, pair, k), j), src, ACT.Abs, bias=bias).then_inc(evacuated, 1)
                elif name == "dt_ln":
                    d = delta_of(kind, pair, i)
                    landed(act, "dt", kind, pair, 2 * i + 1)
                    nc.scalar.activation(d, d, ACT.Exp, scale=-1.0).then_inc(K["dt_exp"][kind], 1)
                    act.wait_ge(K["dt_exp"][kind], 3 * pair + nth(i))
                    nc.scalar.activation(d, d, ACT.Ln, bias=1.0).then_inc(K["dt_logged"][kind], 1)
                elif name == "w_out":
                    src = full(unit)[0:C, :]
                    if kind == ROWS:
                        nc.scalar.activation(half(x1[:, k, :], j), src, ACT.Copy)
                        nc.scalar.activation(half(squares(k), j), src, ACT.Square).then_inc(evacuated, 1)
                    else:
                        nc.scalar.activation(half(io[:, k, :], j), src, ACT.Copy).then_inc(evacuated, 1)
                elif name == "centre":
                    src = full(unit)[0:C, :]
                    nc.scalar.activation(half(x1[:, k, :], j), src, ACT.Identity, bias=b_centre[:, :])
                    nc.scalar.activation(half(squares(k), j), src, ACT.Square, bias=b_centre[:, :]).then_inc(evacuated, 1)
                elif name == "var":
                    c = i % 4
                    nc.scalar.activation(half(squares(c // 2), c % 2), full(unit)[0:C, :], ACT.Copy).then_inc(evacuated, 1)
                elif name == "rstd":
                    landed(act, "var", kind, pair, 4 * i + 3)
                    nc.scalar.activation(xr[0:C, 0:2, :], xr[0:C, 0:2, :], ACT.Ln, bias=eps[:, :]).then_inc(logged, 1)
                    act.wait_ge(logged, 2 * pair + i + 1)
                    nc.scalar.activation(xr[0:C, 0:2, :], xr[0:C, 0:2, :], ACT.Exp, scale=-0.5).then_inc(rstd_done, 1)
                elif name == "affine":
                    act.wait_ge(norm_done, 4 * pair + 2 + i + 1)
                    ln = col("ln")
                    nc.scalar.activation(x1[:, i, :], x1[:, i, :], ACT.Identity, scale=ln[0:C, 2:3],
                                         bias=ln[0:C, 3:4]).then_inc(affine_done, 1)

            act.wait_ge(s_centre, 1)
            nc.scalar.activation(b_centre[:, :], bank[0:C, 0, 0:1], ACT.Copy).then_inc(s_centre, 1)
            walk(("ahead", "jobs"), job, ahead=look_ahead)

        @block.vector
        def _(dve):
            dve.wait_ge(s_w, 32)
            nc.vector.memset(eps[:, :], EPS)
            nc.vector.tensor_copy(sel[:, :, :], col("sel")[0:C, :].rearrange("p (b n) -> p b n", b=2)).then_inc(s_sel, 1)
            dve.wait_ge(s_sel, 1)
            for b in range(2):
                last = nc.vector.tensor_copy(sel_m[:, :, b, :],
                                             sel[:, b, :].rearrange("p (n o) -> p n o", o=1).to_broadcast([C, NS, P // 2]))
            last.then_inc(s_const, 1)
            for layer in range(2):
                f = ring[0:DT_ROWS, layer, 0:3 * P]
                hi = ring[0:DT_ROWS, 2 + layer, 0:3 * P // 2].bitcast(bf16)
                part = w_dt[:, layer, :, :].rearrange("p k c -> p (k c)")
                masks = col("split")[0:DT_ROWS, :]
                nc.vector.tensor_copy(hi, f).then_inc(s_split, 1)
                dve.wait_ge(s_split, 4 * layer + 1)
                nc.vector.scalar_tensor_tensor(out=f, in0=hi, scalar=masks[:, 0:1], in1=f, op0=ALU.mult, op1=ALU.add).then_inc(s_split, 1)
                dve.wait_ge(s_split, 4 * layer + 2)
                nc.vector.tensor_copy(hi, f).then_inc(s_split, 1)
                dve.wait_ge(s_split, 4 * layer + 3)
                nc.vector.scalar_tensor_tensor(out=part, in0=hi, scalar=masks[:, 1:2], in1=f, op0=ALU.mult, op1=ALU.add).then_inc(s_split, 1)
            wo = col("w_out", 0).rearrange("p (v c) -> p v c", v=3)
            nc.vector.tensor_reduce(w_sum[:, :], wo, mybir.AxisListType.X, ALU.add).then_inc(s_sums, 1)
            dve.wait_ge(s_sums, 1)
            nc.vector.tensor_scalar(w_sum[:, :], w_sum[:, :], -1.0 / C, None, ALU.mult).then_inc(s_sums, 1)
            dve.wait_ge(s_sums, 2)
            for v in range(3):
                last = nc.vector.tensor_scalar(wo[:, v, :], wo[:, v, :], w_sum[:, v:v + 1], None, ALU.add)
            last.then_inc(s_sums, 1)
            nc.vector.tensor_scalar(w_centre[:, :], col("centre")[0:C, :], col("ln")[0:C, 0:1], None, ALU.mult)
            dve.wait_ge(s_sums, 3)
            dve.wait_ge(s_nega, 2)
            for layer in range(2):
                w = small[layer][:, :, 0:5]
                nc.vector.tensor_scalar(w, w, 0.5, None, ALU.mult)
                wo = col("w_out", layer)
                nc.vector.tensor_scalar(wo, wo, 0.5, None, ALU.mult)
            last = nc.vector.tensor_scalar(neg_a[:, :, :], neg_a[:, :, :], -1.0, None, ALU.mult)
            last.then_inc(s_const, 1)

            def look_ahead(g):
                if g >= ALL_STEPS:
                    return
                kind, pair, k, n = step_at(g)
                if n == 0:
                    dve.wait_ge(K["set_ready"][kind], 3 * pair + nth(k))
                wait(dve, g_summed, g - RING + 1)
                dve.wait_ge(b_ready, g + 1)
                nc.vector.tensor_tensor(ring[:, g % RING, :], u_of(kind, pair, k), b_ps[:, :], ALU.mult).then_inc(b_used, 1)

            def take(tile):
                it = ITEMS[tile // TILES]
                kind, pair, k = it["kind"], it["pair"], tile % TILES
                dve.wait_ge(K["skip_done"][kind], 3 * pair + k + 1)
                if kind == FWD:
                    dve.wait_ge(K["skip_done"][BWD], 3 * pair + k + 1)
                if kind == BWD:
                    dve.wait_ge(y_taken, 2 * (tile - TILES + 1))
                dve.wait_ge(g_summed, NS * (tile + 1))
                for j in range(2):
                    y = half(yv_of(kind, pair, k), j)
                    nc.vector.tensor_tensor(y, y, half(y_ps[:, :], j), ALU.add).then_inc(y_taken, 1)

            def slot_begin(g):
                if g % NS == SUM_LAG and g >= NS:
                    take(g // NS - 1)

            def slot_mid(g):
                kind, pair, k, n = step_at(g)
                dve.wait_ge(a_ready, g + 1)
                dve.wait_ge(b_used, g + 1)
                a, h = a_ring[:, g % A_RING, :], ring[:, g % RING, :]
                if kind == BWD:
                    a, h = a[:, ::-1], h[:, ::-1]
                nc.vector.tensor_tensor_scan(out=h, data0=a, data1=h, initial=0.0,
                                             op0=ALU.mult, op1=ALU.add).then_inc(h_ready, 1)

            def slot_end(g):
                if g == ALL_STEPS - 1:
                    take(g // NS)

            def job(name, kind, pair, i, unit, use):
                layer = LAYER[kind]
                k, j = i // 2, i % 2
                sm = small[layer]
                if name == "conv":
                    k, m = i // 3, i % 3
                    d = TAPS - 1 - m
                    if m == 0 and kind == BWD:
                        dve.wait_ge(xr_ready, 6 * pair + 2 * (k + 1))
                    elif m == 0:
                        landed(dve, "xr", kind, pair, 2 * k + 1)
                    else:
                        dve.wait_ge(K["conv_done"][kind], 9 * pair + i)
                    acc, src = xs[:, k, :], xr[:, k, :]
                    if kind == ROWS:
                        acc = acc.rearrange("p (s t) -> p s t", t=W)[:, :, d:W]
                        src = src.rearrange("p (s t) -> p s t", t=W)[:, :, 0:W - d]
                    elif kind == FWD:
                        acc, src = acc[:, d:T], src[:, 0:T - d]
                    else:
                        acc, src = acc[:, 0:T - d], src[:, d:T]
                    nc.vector.scalar_tensor_tensor(out=acc, in0=src, scalar=sm[:, m_of(k), m:m + 1], in1=acc,
                                                   op0=ALU.mult, op1=ALU.add).then_inc(K["conv_done"][kind], 1)
                elif name in ("silu", "gate"):
                    q = use_of[made[name], kind, pair, i]
                    dve.wait_ge(th_ready, q + 1)
                    if name == "gate":
                        landed(dve, "z", kind, pair, i)
                    v = half(xs[:, k, :] if name == "silu" else sz_of(kind, pair, k), j)
                    nc.vector.scalar_tensor_tensor(out=v, in0=th[:, q % 2, :], scalar=1.0, in1=v,
                                                   op0=ALU.add, op1=ALU.mult).then_inc(th_used, 1)
                elif name == "skip" and kind == BWD:
                    dve.wait_ge(K["skip_done"][FWD], 3 * pair + i + 1)
                    halved(dve, "silu", kind, pair, 2 * i + 1)
                    y = yv_of(kind, pair, i)
                    nc.vector.scalar_tensor_tensor(out=y, in0=xs[:, i, :], scalar=sm[:, m_of(i), 6:7], in1=y,
                                                   op0=ALU.mult, op1=ALU.add).then_inc(K["skip_done"][kind], 1)
                elif name == "split_hi":
                    landed(dve, "dbl", kind, pair, i)
                    v = dbl[:, i, :]
                    nc.vector.tensor_tensor(v, v, parts3[:, i, 0, :], ALU.subtract).then_inc(K["hi_done"][kind], 1)
                elif name == "split_lo":
                    dve.wait_ge(K["mid_ready"][kind], 2 * pair + i + 1)
                    nc.vector.tensor_tensor(parts3[:, i, 2, :], dbl[:, i, :], parts3[:, i, 1, :],
                                            ALU.subtract).then_inc(K["lo_done"][kind], 1)

            walk(DVE_ORDER, job, ahead=look_ahead, take=slot_begin, scan=slot_mid, last=slot_end)

        @block.gpsimd
        def _(pool):
            def slot_mid(g):
                pool.wait_ge(h_ready, g + 1)
                pool.wait_ge(c_copied, g + 1)
                r = ring[:, g % RING, :]
                nc.gpsimd.tensor_tensor(r, r, c_ring[:, g % C_RING, :], ALU.mult).then_inc(g_ready, 1)

            def job(name, kind, pair, i, unit, use):
                if name == "u":
                    d, u = delta_of(kind, pair, i), u_of(kind, pair, i)
                    pool.wait_ge(K["dt_logged"][kind], 3 * pair + nth(i))
                    nc.gpsimd.tensor_tensor(d, d, u, ALU.add).then_inc(K["dt_added"][kind], 1)
                    pool.wait_ge(K["dt_added"][kind], 3 * pair + nth(i))
                    if kind != ROWS:
                        nc.gpsimd.tensor_tensor(u, d, xs[:, i, :], ALU.mult).then_inc(K["set_ready"][kind], 1)
                        return
                    nc.gpsimd.tensor_tensor(u, d, xs[:, i, :], ALU.mult).then_inc(u_done, 1)
                    pool.wait_ge(u_done, 3 * pair + nth(i))
                    starts = d.rearrange("p (s t) -> p s t", t=W)[:, :, 0:1]
                    nc.gpsimd.memset(starts, BIG).then_inc(K["set_ready"][kind], 1)
                elif name == "gated":
                    pool.wait_ge(y_taken, 2 * (tile_of(kind, pair) + i + 1))
                    halved(pool, "gate", ROWS if kind == ROWS else FWD, pair, 5)
                    y = yv_of(kind, pair, i)
                    nc.gpsimd.tensor_tensor(y, y, sz_of(kind, pair, i), ALU.mult).then_inc(gated_done[kind], 1)
                elif name == "norm":
                    r, b = i // 2, i % 2
                    pool.wait_ge(rstd_done, 2 * pair + r + 1)
                    nc.gpsimd.tensor_tensor(x1[:, b, :], x1[:, b, :], squares(b), ALU.mult).then_inc(norm_done, 1)

            def tile_of(kind, pair):
                return TILES * ordinal[kind, pair]

            walk(("product", "jobs"), job, product=slot_mid)


def pack(inputs):
    wp = np.zeros((P, NCOL), np.float32)

    def put(name, layer, a, row=0, at=0):
        c = _cols[name, layer][0] + at
        wp[row:row + a.shape[0], c:c + a.shape[1]] = a

    for layer, pre in enumerate(("L0_conv_", "L1_conv_")):
        g = lambda n: np.asarray(inputs[pre + n])
        w_in, w_x, w_dt, w_out = g("W_in"), g("W_x" if layer == 0 else "W_xproj"), g("W_dt"), g("W_out")
        for name, w in (("w_xr", w_in[:, :DI]), ("w_z", w_in[:, DI:])):
            put(name, layer, w[:, :P])
            put(name, layer, w[:, P:], 0, P)
            put(name, layer, w[:, P:], 0, 2 * P + DM)
        bb, cc, dt = w_x[:, RANK:RANK + NS], w_x[:, RANK + NS:], w_x[:, :RANK]
        for b in range(2):
            for at, w in ((NS * b, bb), (NS * (2 + b), cc), (BC_ROWS + RANK * b, dt)):
                put("w_dbl", layer, w[:P], 0, b * X_ROWS + at)
                put("w_dbl", layer, w[P:], b * DM, 2 * X_ROWS + at)
            for q in range(len(DT_TERMS)):
                put("w_dt", layer, w_dt[:, :P], RANK * (2 * q + b), b * P)
                put("w_dt", layer, w_dt[:, P:], RANK * (2 * q + b), 2 * P + b * DM)
        put("w_out", layer, w_out[:P])
        put("w_out", layer, w_out[P:], 0, C)
        put("w_out", layer, w_out[P:], DM, 2 * C)
        rows = np.concatenate([g("conv_w").reshape(DI, TAPS), g("conv_b")[:, None], g("b_dt")[:, None], g("D")[:, None]], axis=1)
        for name, a in (("small", rows), ("a_log", g("A_log"))):
            put(name, layer, a[:P])
            put(name, layer, a[P:], 0, a.shape[1])
            put(name, layer, a[P:], DM, a.shape[1])
        put("ln", None, np.stack([g("ln_g"), g("ln_b")], axis=1), 0, 2 * layer)
    put("ident", None, np.eye(P, dtype=np.float32))
    put("mean", None, np.full((C, C), 1.0 / C, np.float32))
    sel = np.zeros((C, 2, NS), np.float32)
    for b in range(2):
        for g in range(3):
            for n in range(NS):
                sel[(g * 2 + b) * NS + n, b, n] = 1.0
    split = np.zeros((DT_ROWS, 2), np.float32)
    for q, (_, g) in enumerate(DT_TERMS):
        split[2 * RANK * q:2 * RANK * (q + 1)] = (-1.0 if g >= 1 else 0.0, -1.0 if g == 2 else 0.0)
    put("centre", None, np.eye(C, dtype=np.float32) - np.full((C, C), 1.0 / C, np.float32))
    put("sel", None, sel.reshape(C, 2 * NS))
    put("split", None, split)
    return wp


def kernel(**inputs):
    import concourse.bacc as bacc
    from concourse.bass_utils import run_bass_kernel_spmd

    nc = bacc.Bacc("TRN2", target_bir_lowering=False, num_devices=1)
    arrays = {"x": np.ascontiguousarray(np.asarray(inputs["x"]).reshape(B, C, T)), "wpack": pack(inputs)}
    x = nc.dram_tensor("x", (B, C, T), mybir.dt.float32, kind="ExternalInput").ap()
    wpack = nc.dram_tensor("wpack", (P, NCOL), mybir.dt.float32, kind="ExternalInput").ap()
    out = nc.dram_tensor("out", (B, C, T), mybir.dt.float32, kind="ExternalOutput").ap()
    build_program(nc, x, wpack, out)
    r = run_bass_kernel_spmd(nc, [arrays], core_ids=[0])
    return r.results[0]["out"].reshape(B, C, H, W)
```

```python
import numpy as np
import concourse.bass as bass
from concourse import mybir
from contextlib import ExitStack

B, C, H, W = 8, 96, 32, 32
T = H * W
DI = 2 * C
NS = 16
RANK = C // 16
TAPS = 4
P = 128
DM = DI - P
PAIRS = B // 2
HALF = T // 2
BIG = 1.0e34
EPS = 1e-5

ROWS, FWD, BWD = "rows", "fwd", "bwd"
LAYER = {ROWS: 0, FWD: 1, BWD: 1}
TILES = 3
BC_ROWS = 4 * NS
X_ROWS = BC_ROWS + 2 * RANK
DT_TERMS = ((0, 0), (0, 1), (1, 0), (1, 1), (0, 2), (2, 0))
DT_ROWS = 2 * RANK * len(DT_TERMS)
STEPS = TILES * NS
RING = 4
C_RING = 4
A_RING = 3

_cols, _at = {}, 0
for _name, _n in [("w_xr", 3 * P), ("w_z", 3 * P), ("w_dbl", 3 * X_ROWS), ("w_out", 3 * C),
                  ("small", 2 * 7), ("a_log", 2 * NS)]:
    for _layer in range(2):
        _cols[_name, _layer] = (_at, _n)
        _at += _n
for _name, _n in [("ident", P), ("mean", C), ("centre", C), ("sel", 2 * NS), ("split", 2), ("ln", 4)]:
    _cols[_name, None] = (_at, _n)
    _at += _n
NKEPT = _at
for _layer in range(2):
    _cols["w_dt", _layer] = (_at, 3 * P)
    _at += 3 * P
NCOL = _at


PE_ORDER = ("ahead", "ahead_c", "sum_0", "jobs", "sum_1")
ACT_ORDER = ("ahead_c", "ahead_a", "jobs")
DVE_ORDER = ("take_0", "scan", "take_1", "ahead", "jobs", "last")
LEAD = {"ahead": 1, "ahead_c": 2, "ahead_a": 2}
SUM_LAG = 2


def fills_prep(kind, pair, at=None):
    at = at or PREP
    out = []
    for u in range(6):
        out.append((at["xr"][u], "xr", u))
    for k in range(TILES):
        for m in range(TAPS - 1):
            out.append((at["conv"][k] + m, "conv", 3 * k + m))
        for j in range(2):
            out.append((at["tanh"][k] + j, "tanh", 2 * k + j))
            out.append((at["tanh"][k] + 1 + j, "silu", 2 * k + j))
        out.append((at["skip"][k], "skip", k))
    for j in range(2):
        for n, name in enumerate(("dbl", "split_hi", "split_mid", "split_lo")):
            out.append((at["dbl"][j] + n, name, j))
    out.append((at["dbl"][1] + 4, "bc_in", 0))
    for u in range(6):
        out.append((at["dt"][u], "dt", u))
    for k in range(TILES):
        out.append((at["exp"][k], "dt_exp", k))
        out.append((at["ln"][k], "dt_ln", k))
        out.append((at["u"][k], "u", k))
    if kind != BWD:
        for u in range(6):
            out.append((at["z"][u], "z", u))
            out.append((at["z"][u] + 1, "gate", u))
    return [(s, name, kind, pair, i) for s, name, i in sorted(out, key=lambda x: x[0])]


def fills_post(kind, pair, at=None):
    t = at or POST[kind]
    out = [(t["gated"][k], "gated", k) for k in range(TILES)]
    out += [(t["w_out"][c], "w_out", c) for c in range(4)]
    if kind == ROWS:
        out += [(t["centre"][c], "centre", c) for c in range(4)]
        out += [(t["var"][c], "var", c) for c in range(8)]
        out += [(t["log"][i], "log", i) for i in range(4)]
        out += [(t["rstd"][i], "rstd", i) for i in range(4)]
        out += [(t["norm"][i], "norm", i) for i in range(4)]
        out += [(t["affine"][i], "affine", i) for i in range(2)]
    return [(s, name, kind, pair, i) for s, name, i in sorted(out, key=lambda x: x[0])]


PREP = dict(xr=(0, 1, 2, 2, 5, 5), conv=(2, 4, 6), tanh=(5, 7, 9), skip=(12, 15, 15), dbl=(12, 15),
            dt=(20, 21, 32, 32, 26, 24), exp=(24, 36, 29), ln=(28, 37, 31), u=(29, 40, 32),
            z=(15, 17, 17, 19, 20, 21))
POST = {ROWS: dict(gated=(2, 2, 7), w_out=(9, 9, 11, 14), var=(15, 15, 17, 18, 33, 34, 35, 35),
                   log=(30, 30, 38, 39), rstd=(31, 31, 42, 44), norm=(31, 31, 43, 44), centre=(33, 33, 33, 34),
                   affine=(44, 46)),
        BWD: dict(gated=(0, 2, 4), w_out=(7, 7, 7, 9))}
LATER = {"skip": (0, 1, 2), "dt": {4: 1, 5: 2, 2: 6, 3: 7},
         "dt_exp": {2: 3, 1: 9}, "dt_ln": {2: 3, 1: 9}, "u": {2: 4, 1: 10}}
LATER_Z = (11, 15, 17, 24, 35, 35)
SECOND_ROWS = dict(xr=(12, 13, 14, 14, 15, 16), conv=(13, 15, 17), tanh=(15, 17, 19), skip=(26, 28, 30),
                   dbl=(23, 24), dt=(31, 32, 38, 39, 32, 33), exp=(32, 40, 33), ln=(32, 42, 33),
                   u=(32, 42, 34), z=(36, 38, 39, 40, 40, 43))
FAST_POST = dict(gated=(1, 2, 4), w_out=(6, 7, 9, 9), var=(7, 9, 9, 9, 17, 18, 20, 21), log=(9, 11, 20, 21),
                 rstd=(11, 13, 22, 22), norm=(11, 13, 22, 24), centre=(14, 14, 16, 16), affine=(23, 26))
FIRST_IMAGE = dict(xr=(28, 28, 30, 30, 31, 32), conv=(28, 30, 33), tanh=(31, 33, 35), skip=(42, 43, 45),
                   dbl=(38, 39), dt=(44, 45, 47, 49, 45, 46), exp=(46, 49, 48), ln=(48, 53, 48),
                   u=(58, 60, 59), z=(4, 4, 5, 6, 7, 8))
CONSTANTS = 18.5

BANKED = {"constants", "xr", "z", "dbl", "dt", "w_out", "centre", "var"}


def plan():
    def item(kind, pair, *fills):
        slots = [[] for _ in range(STEPS)]
        for f in fills:
            for s, *job in f:
                slots[s].append(tuple(job))
        return {"kind": kind, "pair": pair, "slots": slots}

    def alone(*fills):
        jobs = sorted((x for f in fills for x in f), key=lambda x: x[0])
        return {"kind": None, "slots": [[tuple(x[1:]) for x in jobs]]}

    load = lambda pair, slot: [(slot, "load", ROWS, pair, 0)]
    z_jobs = lambda fills, them: [x for x in fills if (x[1] in ("z", "gate")) == them]
    now, later = load(0, -2) + load(1, -1) + [(CONSTANTS, "constants", ROWS, 0, 0)], []
    first = dict(PREP, xr=(0, 1, 2, 3, 4, 5), conv=(2, 4, 6), tanh=(5, 7, 9), dbl=(12, 13), z=LATER_Z)
    for s, name, kind, pair, i in fills_prep(ROWS, 0, first):
        if name in ("z", "gate"):
            later.append((s, name, kind, pair, i))
        elif name == "skip" or name in LATER and i in LATER[name]:
            later.append((LATER[name][i], name, kind, pair, i))
        else:
            now.append((s, name, kind, pair, i))
    later.sort(key=lambda x: x[0])
    second = fills_prep(ROWS, 1, SECOND_ROWS)
    image = z_jobs(fills_prep(FWD, 0, FIRST_IMAGE), False)
    first_z = z_jobs(fills_prep(FWD, 0, FIRST_IMAGE), True)
    parts = [
        alone(now),
        item(ROWS, 0, later, second),
        item(ROWS, 1, fills_post(ROWS, 0, FAST_POST), [x for x in image if x[0] < STEPS]),
        alone([x for x in image if x[0] >= STEPS]),
    ]
    for p in range(1, PAIRS):
        if p > 1:
            parts.append(item(ROWS, p, fills_post(BWD, p - 2), fills_prep(FWD, p - 1)))
        fills = [fills_post(ROWS, p), fills_prep(BWD, p - 1)]
        if p == 1:
            fills.insert(0, first_z)
        if p + 1 < PAIRS:
            fills.append(load(p + 1, 20))
        parts.append(item(FWD, p - 1, *fills))
        parts.append(item(BWD, p - 1, fills_prep(ROWS, p + 1) if p + 1 < PAIRS else fills_prep(FWD, p)))
    parts.append(item(FWD, PAIRS - 1, fills_post(BWD, PAIRS - 2), fills_prep(BWD, PAIRS - 1)))
    parts.append(item(BWD, PAIRS - 1))
    parts.append(alone(fills_post(BWD, PAIRS - 1)))
    step = unit = use = 0
    for part in parts:
        part["step"] = step
        if part["kind"]:
            step += STEPS
        for slot in part["slots"]:
            for n, (name, kind, pair, i) in enumerate(slot):
                takes = name in BANKED and not (name == "xr" and kind == BWD)
                tanh = name in ("tanh", "z")
                slot[n] = (name, kind, pair, i, unit if takes else None, use if tanh else None)
                unit += takes
                use += tanh
    return parts


def build_program(nc, x, wpack, out):
    f32, bf16 = mybir.dt.float32, mybir.dt.bfloat16
    ALU, ACT = mybir.AluOpType, mybir.ActivationFunctionType
    PARTS = plan()
    ITEMS = [p for p in PARTS if p["kind"]]
    ALL_STEPS = STEPS * len(ITEMS)

    with ExitStack() as ctx:
        sb = lambda name, shape, dt=f32: ctx.enter_context(nc.sbuf_tensor(name, shape, dt))
        ps = lambda name, shape: ctx.enter_context(nc.psum_tensor(name, shape, f32))
        sem = lambda name: ctx.enter_context(nc.semaphore(name))

        wp = sb("wp", [P, NKEPT])
        sel = sb("sel", [C, 2, NS], bf16)
        sel_m = sb("sel_m", [C, NS, 2, P // 2], bf16)
        io = sb("io", [C, 2, T])
        x1 = sb("x1", [C, 2, T])
        xr = sb("xr", [P, TILES, T])
        xs = sb("xs", [P, TILES, T])
        th = sb("th", [P, 2, HALF])
        yv = {k: sb(f"yv_{k}", [P, TILES, T]) for k in (ROWS, FWD)}
        sz = {k: sb(f"sz_{k}", [P, TILES, T]) for k in (ROWS, FWD)}
        delta_ab = sb("delta_ab", [P, 2, T])
        u_ab = sb("u_ab", [P, 2, T])
        delta_m = sb("delta_m", [P, 2, T])
        u_m = sb("u_m", [P, 2, T])
        b_in = sb("b_in", [C, 2, T], bf16)
        c_in = sb("c_in", [C, 2, T], bf16)
        dbl = sb("dbl", [X_ROWS, 2, HALF])
        parts3 = sb("parts3", [X_ROWS, 2, 3, HALF], bf16)
        dt_in = sb("dt_in", [DT_ROWS, T], bf16)
        w_dt = sb("w_dt_parts", [DT_ROWS, 2, 3, P], bf16)
        w_centre = sb("w_centre", [C, C])
        b_centre = sb("b_centre", [C, 1])
        w_sum = sb("w_sum", [P, 3])
        ring = sb("ring", [P, RING, T])
        c_ring = sb("c_ring", [P, C_RING, T])
        a_ring = sb("a_ring", [P, A_RING, T])
        eps = sb("eps", [C, 1])
        neg_a = sb("neg_a", [P, 2, 2 * NS])
        b_ps = ps("b_ps", [P, 2, T])
        y_ps = ps("y_ps", [P, T])
        bank = ps("bank", [P, 2, HALF])

        def col(name, layer=None):
            at, n = _cols[name, layer]
            return wp[:, at:at + n]

        ident = col("ident")
        small = [col("small", l).rearrange("p (m c) -> p m c", m=2) for l in range(2)]
        ordinal = {(it["kind"], it["pair"]): n for n, it in enumerate(ITEMS)}
        parity = lambda kind, pair: ordinal[kind, pair] % 2
        delta_of = lambda kind, pair, k: delta_ab[:, k, :] if k < 2 else delta_m[:, parity(kind, pair), :]
        u_of = lambda kind, pair, k: u_ab[:, k, :] if k < 2 else u_m[:, parity(kind, pair), :]

        def y_name(kind, pair):
            if kind == ROWS:
                return FWD if pair == 0 else ROWS
            return ROWS if pair == PAIRS - 1 else FWD

        yv_of = lambda kind, pair, k: yv[y_name(kind, pair)][:, k, :]
        sz_of = lambda kind, pair, k: sz[y_name(kind, pair)][:, k, :]
        half = lambda ap, j: ap[:, j * HALF:(j + 1) * HALF]
        m_of = lambda k: 0 if k < 2 else 1
        squares = lambda b: xr[0:C, b, :]

        s_sel, s_w, s_const, s_nega = sem("sel_made"), sem("weights_in"), sem("constants_ready"), sem("a_made")
        s_halved = sem("small_halved")
        b_ready, b_used = sem("b_ready"), sem("b_used")
        c_ready, c_copied = sem("c_ready"), sem("c_copied")
        a_ready, h_ready = sem("a_ready"), sem("h_ready")
        g_ready, g_summed, y_taken = sem("g_ready"), sem("g_summed"), sem("y_taken")
        produced, evacuated = sem("bank_produced"), sem("bank_evacuated")
        K = {n: {k: sem(f"{n}_{k}") for k in LAYER} for n in (
            "conv_done", "skip_done", "hi_done", "mid_ready", "lo_done", "bc_loaded", "dt_loaded",
            "dt_exp", "dt_logged", "dt_added", "set_ready")}
        xr_ready, u_done = sem("xr_ready_bwd"), sem("u_done_rows")
        th_ready, th_used = sem("tanh_ready"), sem("tanh_used")
        gated_done = {k: sem(f"gated_done_{k}") for k in (ROWS, BWD)}
        x_loaded = [sem(f"x_loaded_{i}") for i in range(2)]
        out_stored, logged, rstd_done, norm_done = sem("out_stored"), sem("logged"), sem("rstd_done"), sem("norm_done")
        affine_done, s_split, s_sums = sem("affine_done"), sem("w_dt_split"), sem("w_sums")

        unit_of = {j[:4]: j[4] for p in PARTS for slot in p["slots"] for j in slot}

        units_before, c_before, units, steps_c = [], [], 0, 0
        for n, part in enumerate(PARTS):
            if part["kind"] and n and not PARTS[n - 1]["kind"]:
                units_before += [units] * LEAD["ahead_c"]
                steps_c += LEAD["ahead_c"]
            for s, slot in enumerate(part["slots"]):
                if part["kind"] and (s + LEAD["ahead_c"] < STEPS or PARTS[n + 1]["kind"]):
                    units_before.append(units)
                    steps_c += 1
                for j in slot:
                    if j[4] is not None:
                        c_before.append(steps_c)
                        units += 1
        use_of = {j[:4]: j[5] for p in PARTS for slot in p["slots"] for j in slot}
        made = {"silu": "tanh", "gate": "z"}
        order = [use_of[made[j[0]], *j[1:4]] for p in PARTS for slot in p["slots"] for j in slot if j[0] in made]
        assert order == sorted(order)

        def halved(eng, name, kind, pair, i):
            eng.wait_ge(th_used, use_of[made[name], kind, pair, i] + 1)

        def landed(eng, name, kind, pair, i):
            eng.wait_ge(evacuated, unit_of[name, kind, pair, i] + 1)

        ready_order = {k: sorted(range(TILES), key=lambda t: (PREP["u"][t], t)) for k in LAYER}
        nth = lambda k: ready_order[ROWS].index(k) + 1

        def source(kind, pair):
            return x1 if kind != ROWS or pair == 1 else io

        BC_LOADS, DT_LOADS = 16 * 6, 16 * len(DT_TERMS)

        block = ctx.enter_context(nc.Block())

        def wait(eng, s, value):
            if value > 0:
                eng.wait_ge(s, value)

        def step_at(g):
            it = ITEMS[g // STEPS]
            s = g % STEPS
            return it["kind"], it["pair"], s // NS, s % NS

        def walk(order, job, **phases):
            for n, part in enumerate(PARTS):
                if not part["kind"]:
                    for j in part["slots"][0]:
                        job(*j)
                    continue
                g0 = part["step"]
                if n and not PARTS[n - 1]["kind"]:
                    for phase in order:
                        if phase in LEAD:
                            for g in range(LEAD[phase]):
                                phases[phase](g0 + g)
                for s in range(STEPS):
                    for phase in order:
                        if phase == "jobs":
                            for j in part["slots"][s]:
                                job(*j)
                        elif phase in LEAD:
                            if s + LEAD[phase] < STEPS or PARTS[n + 1]["kind"]:
                                phases[phase](g0 + s + LEAD[phase])
                        else:
                            phases[phase](g0 + s)

        @block.sync
        def _(sp):
            sp.dma_start(wp[:, :], wpack[:, 0:NKEPT]).then_inc(s_w, 16)
            sp.dma_start(ring[0:DT_ROWS, 0:2, 0:3 * P],
                         wpack[0:DT_ROWS, NKEPT:].rearrange("p (l c) -> p l c", l=2)).then_inc(s_w, 16)

            def job(name, kind, pair, i, unit, use):
                if name == "load":
                    dst = source(kind, pair)
                    if pair > 1:
                        if pair > 2:
                            landed(sp, "z", ROWS, pair - 1, 5)
                        wait(sp, out_stored, 64 * (pair - 2))
                    for b in range(2):
                        sp.dma_start(dst[:, b, :], x[2 * pair + b]).then_inc(x_loaded[pair % 2], 16)
                elif name == "bc_in":
                    sp.wait_ge(K["lo_done"][kind], 2 * (pair + 1))
                    both = lambda dst: dst.rearrange("p (j t) -> p j t", j=2)
                    for q, (g, _) in enumerate(DT_TERMS):
                        sp.dma_start(both(dt_in[2 * RANK * q:2 * RANK * (q + 1), :]),
                                     parts3[BC_ROWS:X_ROWS, :, g, :]).then_inc(K["dt_loaded"][kind], 16)
                    rows = 2 * NS
                    for g in range(3):
                        for dst, at in ((b_in, 0), (c_in, rows)):
                            sp.dma_start(both(dst[rows * g:rows * (g + 1), parity(kind, pair), :]),
                                         parts3[at:at + rows, :, g, :]).then_inc(K["bc_loaded"][kind], 16)
                elif name == "w_out" and kind == BWD:
                    b, j = i // 2, i % 2
                    landed(sp, name, kind, pair, i)
                    sp.dma_start(half(out[2 * pair + b], j), half(io[:, b, :], j)).then_inc(out_stored, 16)

            walk(("jobs",), job)
            sp.wait_ge(out_stored, 64 * PAIRS)

        @block.tensor
        def _(pe):
            pe.wait_ge(s_w, 32)

            def pick(k, n):
                if k < 2:
                    return sel[:, k, n:n + 1].to_broadcast([C, P])
                return sel_m[:, n, :, :].rearrange("p b c -> p (b c)")

            def look_ahead(g):
                if g >= ALL_STEPS:
                    return
                kind, pair, k, n = step_at(g)
                if g % STEPS == 0:
                    pe.wait_ge(K["bc_loaded"][kind], BC_LOADS * (pair + 1))
                wait(pe, h_ready, g - 1)
                for j in range(2):
                    last = nc.tensor.matmul(half(b_ps[:, g % 2, :], j), pick(k, n), half(b_in[:, parity(kind, pair), :], j), start=True, stop=True)
                last.then_inc(b_ready, 1)

            def look_ahead_c(g):
                if g >= ALL_STEPS:
                    return
                kind, pair, k, n = step_at(g)
                if g % STEPS == 0:
                    pe.wait_ge(K["bc_loaded"][kind], BC_LOADS * (pair + 1))
                wait(pe, c_copied, g)
                for j in range(2):
                    wait(pe, evacuated, units_before[g] - (units_before[g] + j + 1) % 2)
                    last = nc.tensor.matmul(bank[:, j, :], pick(k, n), half(c_in[:, parity(kind, pair), :], j), start=True, stop=True)
                last.then_inc(c_ready, 1)

            def sum_half(g, j):
                n = g % NS
                pe.wait_ge(g_ready, g + 1)
                if n == 0:
                    wait(pe, y_taken, 2 * (g // NS - 1) + j + 1)
                nc.tensor.matmul(half(y_ps[:, :], j), ident, half(ring[:, g % RING, :], j),
                                 start=(n == 0), stop=(n == NS - 1)).then_inc(g_summed, 1)

            def sum_0(g):
                if g >= SUM_LAG:
                    sum_half(g - SUM_LAG, 0)

            def sum_1(g):
                if g >= SUM_LAG:
                    sum_half(g - SUM_LAG, 1)
                if g == ALL_STEPS - 1:
                    for left in range(g - SUM_LAG + 1, g + 1):
                        for j in range(2):
                            sum_half(left, j)

            def product(unit, rows, terms):
                wait(pe, evacuated, unit - 1)
                wait(pe, c_copied, c_before[unit])
                for n, (w, m) in enumerate(terms):
                    last = nc.tensor.matmul(bank[0:rows, unit % 2, :], w, m, start=(n == 0), stop=(n == len(terms) - 1))
                last.then_inc(produced, 1)

            def by_batch(name, layer, rows=P):
                w = col(name, layer).rearrange("p (v c) -> p v c", v=3)
                return [w[0:rows, v, :] for v in range(3)]

            def job(name, kind, pair, i, unit, use):
                layer = LAYER[kind]
                k, j = i // 2, i % 2
                if name in ("xr", "z") and unit is not None:
                    src = source(kind, pair)
                    if name == "xr" and i == 0:
                        if kind == ROWS:
                            pe.wait_ge(x_loaded[pair % 2], 32 * (pair // 2 + 1))
                        else:
                            pe.wait_ge(affine_done, 2 * (pair + 1))
                    w = by_batch("w_xr" if name == "xr" else "w_z", layer, C)
                    if k < 2:
                        product(unit, P, [(w[0], half(src[:, k, :], j))])
                    else:
                        product(unit, P, [(w[1 + b], half(src[:, b, :], j)) for b in range(2)])
                elif name == "constants":
                    wait(pe, evacuated, unit - 1)
                    wait(pe, c_copied, c_before[unit])
                    nc.tensor.matmul(bank[0:C, unit % 2, 0:1], col("centre")[0:C, :], col("ln")[0:C, 1:2],
                                     start=True, stop=True).then_inc(produced, 1)
                    pe.wait_ge(s_const, 1)
                elif name == "dbl":
                    halved(pe, "silu", kind, pair, 5)
                    w = by_batch("w_dbl", layer)
                    product(unit, X_ROWS, [(w[k], half(xs[:, k, :], i)) for k in range(TILES)])
                elif name == "dt":
                    pe.wait_ge(K["dt_loaded"][kind], DT_LOADS * (pair + 1))
                    product(unit, P, [(w_dt[:, layer, k, :], half(dt_in[:, :], j))])
                elif name == "w_out":
                    pe.wait_ge(gated_done[kind], 3 * (pair + 1))
                    w = by_batch("w_out", layer)
                    product(unit, C, [(w[0], half(yv_of(kind, pair, k), j)), (w[1 + k], half(yv_of(kind, pair, 2), j))])
                elif name == "centre":
                    pe.wait_ge(norm_done, 4 * pair + k + 1)
                    product(unit, C, [(w_centre[:, :], half(x1[:, k, :], j))])
                elif name == "var":
                    c = i % 4
                    landed(pe, "w_out" if i < 4 else "centre", kind, pair, c)
                    product(unit, C, [(col("mean")[0:C, :], half(squares(c // 2), c % 2))])

            walk(PE_ORDER, job, ahead=look_ahead, ahead_c=look_ahead_c, sum_0=sum_0, sum_1=sum_1)

        @block.scalar
        def _(act):
            act.wait_ge(s_w, 32)
            for layer in range(2):
                nc.scalar.activation(neg_a[:, layer, :], col("a_log", layer), ACT.Exp).then_inc(s_nega, 1)
            act.wait_ge(s_halved, 1)

            def look_ahead(g):
                if g >= ALL_STEPS:
                    return
                kind, pair, k, n = step_at(g)
                if n == 0:
                    act.wait_ge(K["set_ready"][kind], 3 * pair + nth(k))
                wait(act, h_ready, g - A_RING + 1)
                nc.scalar.activation(a_ring[:, g % A_RING, :], delta_of(kind, pair, k), ACT.Exp,
                                     scale=neg_a[:, LAYER[kind], m_of(k) * NS + n:m_of(k) * NS + n + 1]).then_inc(a_ready, 1)

            def look_ahead_c(g):
                if g >= ALL_STEPS:
                    return
                act.wait_ge(c_ready, g + 1)
                wait(act, g_ready, g - C_RING + 1)
                nc.scalar.activation(c_ring[:, g % C_RING, :], bank[:, :, :].rearrange("p j t -> p (j t)"), ACT.Copy).then_inc(c_copied, 1)

            loaded = [None]

            def table(name):
                if loaded[0] != name:
                    nc.scalar.preload_act_table_set(name)
                    loaded[0] = name

            def full(unit):
                act.wait_ge(produced, unit + 1)
                return bank[:, unit % 2, :]

            def tanh(src, use, **kw):
                table("exp_and_others")
                wait(act, th_used, use - 1)
                return nc.scalar.activation(th[:, use % 2, :], src, ACT.Tanh, **kw).then_inc(th_ready, 1)

            def job(name, kind, pair, i, unit, use):
                layer = LAYER[kind]
                k, j = i // 2, i % 2
                sm = small[layer]
                if name == "xr":
                    src = half(xr[:, k, :], j)
                    if ordinal[kind, pair] and j == 0:
                        before = ITEMS[ordinal[kind, pair] - 1]
                        act.wait_ge(K["set_ready"][before["kind"]], 3 * before["pair"] + nth(k))
                    if unit is not None:
                        src = full(unit)
                        nc.scalar.activation(half(xr[:, k, :], j), src, ACT.Copy)
                    nc.scalar.activation(half(xs[:, k, :], j), src, ACT.Identity, scale=sm[:, m_of(k), 3:4],
                                         bias=sm[:, m_of(k), 4:5]).then_inc(xr_ready if unit is None else evacuated, 1)
                elif name == "tanh":
                    act.wait_ge(K["conv_done"][kind], 9 * pair + 3 * (k + 1))
                    tanh(half(xs[:, k, :], j), use)
                elif name == "skip" and kind != BWD:
                    halved(act, "silu", kind, pair, 2 * i + 1)
                    nc.scalar.activation(yv_of(kind, pair, i), xs[:, i, :], ACT.Identity,
                                         scale=sm[:, m_of(i), 6:7]).then_inc(K["skip_done"][kind], 1)
                elif name == "z":
                    src = full(unit)
                    tanh(src, use, scale=0.5)
                    nc.scalar.activation(half(sz_of(kind, pair, k), j), src, ACT.Copy).then_inc(evacuated, 1)
                elif name == "dbl":
                    src = full(unit)[0:X_ROWS, :]
                    nc.scalar.activation(parts3[:, i, 0, :], src, ACT.Copy)
                    nc.scalar.activation(dbl[:, i, :], src, ACT.Copy).then_inc(evacuated, 1)
                elif name == "constants":
                    nc.scalar.activation(b_centre[:, :], full(unit)[0:C, 0:1], ACT.Copy).then_inc(evacuated, 1)
                    act.wait_ge(s_const, 1)
                elif name == "split_mid":
                    act.wait_ge(K["hi_done"][kind], 2 * pair + i + 1)
                    nc.scalar.activation(parts3[:, i, 1, :], dbl[:, i, :], ACT.Copy).then_inc(K["mid_ready"][kind], 1)
                elif name == "dt":
                    src = full(unit)
                    if k < 2:
                        wait(act, b_used, STEPS * (ordinal[kind, pair] - 1) + NS * (k + 1))
                    bias = sm[:, m_of(k), 5:6]
                    nc.scalar.activation(half(u_of(kind, pair, k), j), src, ACT.Relu, bias=bias)
                    nc.scalar.activation(half(delta_of(kind, pair, k), j), src, ACT.Abs, bias=bias).then_inc(evacuated, 1)
                elif name == "dt_exp":
                    d = delta_of(kind, pair, i)
                    landed(act, "dt", kind, pair, 2 * i + 1)
                    nc.scalar.activation(d, d, ACT.Exp, scale=-1.0).then_inc(K["dt_exp"][kind], 1)
                elif name == "dt_ln":
                    d = delta_of(kind, pair, i)
                    table("natural_log_exp_and_others")
                    act.wait_ge(K["dt_exp"][kind], 3 * pair + nth(i))
                    nc.scalar.activation(d, d, ACT.Ln, bias=1.0).then_inc(K["dt_logged"][kind], 1)
                elif name == "w_out":
                    src = full(unit)[0:C, :]
                    if kind == ROWS:
                        nc.scalar.activation(half(x1[:, k, :], j), src, ACT.Copy)
                        nc.scalar.activation(half(squares(k), j), src, ACT.Square).then_inc(evacuated, 1)
                    else:
                        nc.scalar.activation(half(io[:, k, :], j), src, ACT.Copy).then_inc(evacuated, 1)
                elif name == "centre":
                    src = full(unit)[0:C, :]
                    nc.scalar.activation(half(x1[:, k, :], j), src, ACT.Identity, bias=b_centre[:, :])
                    nc.scalar.activation(half(squares(k), j), src, ACT.Square, bias=b_centre[:, :]).then_inc(evacuated, 1)
                elif name == "var":
                    c = i % 4
                    nc.scalar.activation(half(squares(c // 2), c % 2), full(unit)[0:C, :], ACT.Copy).then_inc(evacuated, 1)
                elif name == "log":
                    b = i % 2
                    table("natural_log_exp_and_others")
                    landed(act, "var", kind, pair, 2 * i + 1)
                    nc.scalar.activation(squares(b), squares(b), ACT.Ln, bias=eps[:, :]).then_inc(logged, 1)
                elif name == "rstd":
                    b = i % 2
                    act.wait_ge(logged, 4 * pair + i + 1)
                    nc.scalar.activation(squares(b), squares(b), ACT.Exp, scale=-0.5).then_inc(rstd_done, 1)
                elif name == "affine":
                    act.wait_ge(norm_done, 4 * pair + 2 + i + 1)
                    ln = col("ln")
                    nc.scalar.activation(x1[:, i, :], x1[:, i, :], ACT.Identity, scale=ln[0:C, 2:3],
                                         bias=ln[0:C, 3:4]).then_inc(affine_done, 1)

            walk(ACT_ORDER, job, ahead_a=look_ahead, ahead_c=look_ahead_c)

        @block.vector
        def _(dve):
            dve.wait_ge(s_w, 32)
            nc.vector.memset(eps[:, :], EPS)
            for layer in range(2):
                w = small[layer][:, :, 0:5]
                last = nc.vector.tensor_scalar(w, w, 0.5, None, ALU.mult)
            last.then_inc(s_halved, 1)

            def constants():
                nc.vector.tensor_copy(sel[:, :, :], col("sel")[0:C, :].rearrange("p (b n) -> p b n", b=2)).then_inc(s_sel, 1)
                dve.wait_ge(s_sel, 1)
                for b in range(2):
                    last = nc.vector.tensor_copy(sel_m[:, :, b, :],
                                                 sel[:, b, :].rearrange("p (n o) -> p n o", o=1).to_broadcast([C, NS, P // 2]))
                last.then_inc(s_sel, 1)
                for layer in range(2):
                    f = ring[0:DT_ROWS, layer, 0:3 * P]
                    hi = ring[0:DT_ROWS, 2 + layer, 0:3 * P // 2].bitcast(bf16)
                    part = w_dt[:, layer, :, :].rearrange("p k c -> p (k c)")
                    masks = col("split")[0:DT_ROWS, :]
                    nc.vector.tensor_copy(hi, f).then_inc(s_split, 1)
                    dve.wait_ge(s_split, 4 * layer + 1)
                    nc.vector.scalar_tensor_tensor(out=f, in0=hi, scalar=masks[:, 0:1], in1=f, op0=ALU.mult, op1=ALU.add).then_inc(s_split, 1)
                    dve.wait_ge(s_split, 4 * layer + 2)
                    nc.vector.tensor_copy(hi, f).then_inc(s_split, 1)
                    dve.wait_ge(s_split, 4 * layer + 3)
                    nc.vector.scalar_tensor_tensor(out=part, in0=hi, scalar=masks[:, 1:2], in1=f, op0=ALU.mult, op1=ALU.add).then_inc(s_split, 1)
                wo = col("w_out", 0).rearrange("p (v c) -> p v c", v=3)
                nc.vector.tensor_reduce(w_sum[:, :], wo, mybir.AxisListType.X, ALU.add).then_inc(s_sums, 1)
                dve.wait_ge(s_sums, 1)
                nc.vector.tensor_scalar(w_sum[:, :], w_sum[:, :], -1.0 / C, None, ALU.mult).then_inc(s_sums, 1)
                dve.wait_ge(s_sums, 2)
                for v in range(3):
                    last = nc.vector.tensor_scalar(wo[:, v, :], wo[:, v, :], w_sum[:, v:v + 1], None, ALU.add)
                last.then_inc(s_sums, 1)
                nc.vector.tensor_scalar(w_centre[:, :], col("centre")[0:C, :], col("ln")[0:C, 0:1], None, ALU.mult)
                dve.wait_ge(s_sums, 3)
                dve.wait_ge(s_nega, 2)
                for layer in range(2):
                    wo = col("w_out", layer)
                    nc.vector.tensor_scalar(wo, wo, 0.5, None, ALU.mult)
                last = nc.vector.tensor_scalar(neg_a[:, :, :], neg_a[:, :, :], -1.0, None, ALU.mult)
                last.then_inc(s_const, 1)

            def look_ahead(g):
                if g >= ALL_STEPS:
                    return
                kind, pair, k, n = step_at(g)
                if n == 0:
                    dve.wait_ge(K["set_ready"][kind], 3 * pair + nth(k))
                dve.wait_ge(b_ready, g + 1)
                b = b_ps[:, g % 2, :]
                nc.vector.tensor_tensor(b, u_of(kind, pair, k), b, ALU.mult).then_inc(b_used, 1)

            def take(tile, j):
                it = ITEMS[tile // TILES]
                kind, pair, k = it["kind"], it["pair"], tile % TILES
                if j == 0:
                    dve.wait_ge(K["skip_done"][kind], 3 * pair + k + 1)
                    if kind == FWD:
                        dve.wait_ge(K["skip_done"][BWD], 3 * pair + k + 1)
                    if kind == BWD:
                        dve.wait_ge(y_taken, 2 * (tile - TILES + 1))
                dve.wait_ge(g_summed, 2 * NS * (tile + 1) - 1 + j)
                y = half(yv_of(kind, pair, k), j)
                nc.vector.tensor_tensor(y, y, half(y_ps[:, :], j), ALU.add).then_inc(y_taken, 1)

            def take_at(g, j):
                if g % NS == SUM_LAG and g >= NS:
                    take(g // NS - 1, j)

            def scan(g):
                kind, pair, k, n = step_at(g)
                dve.wait_ge(a_ready, g + 1)
                dve.wait_ge(b_used, g + 1)
                wait(dve, g_summed, 2 * (g - RING + 1))
                a, b, h = a_ring[:, g % A_RING, :], b_ps[:, g % 2, :], ring[:, g % RING, :]
                if kind == BWD:
                    a, b, h = a[:, ::-1], b[:, ::-1], h[:, ::-1]
                nc.vector.tensor_tensor_scan(out=h, data0=a, data1=b, initial=0.0,
                                             op0=ALU.mult, op1=ALU.add).then_inc(h_ready, 1)

            def take_last(g):
                if g == ALL_STEPS - 1:
                    for j in range(2):
                        take(g // NS, j)

            def job(name, kind, pair, i, unit, use):
                layer = LAYER[kind]
                k, j = i // 2, i % 2
                sm = small[layer]
                if name == "conv":
                    k, m = i // 3, i % 3
                    d = TAPS - 1 - m
                    if m == 0 and kind == BWD:
                        dve.wait_ge(xr_ready, 6 * pair + 2 * (k + 1))
                    elif m == 0:
                        landed(dve, "xr", kind, pair, 2 * k + 1)
                    else:
                        dve.wait_ge(K["conv_done"][kind], 9 * pair + i)
                    acc, src = xs[:, k, :], xr[:, k, :]
                    if kind == ROWS:
                        acc = acc.rearrange("p (s t) -> p s t", t=W)[:, :, d:W]
                        src = src.rearrange("p (s t) -> p s t", t=W)[:, :, 0:W - d]
                    elif kind == FWD:
                        acc, src = acc[:, d:T], src[:, 0:T - d]
                    else:
                        acc, src = acc[:, 0:T - d], src[:, d:T]
                    nc.vector.scalar_tensor_tensor(out=acc, in0=src, scalar=sm[:, m_of(k), m:m + 1], in1=acc,
                                                   op0=ALU.mult, op1=ALU.add).then_inc(K["conv_done"][kind], 1)
                elif name == "constants":
                    constants()
                elif name in ("silu", "gate"):
                    q = use_of[made[name], kind, pair, i]
                    dve.wait_ge(th_ready, q + 1)
                    if name == "gate":
                        landed(dve, "z", kind, pair, i)
                    v = half(xs[:, k, :] if name == "silu" else sz_of(kind, pair, k), j)
                    nc.vector.scalar_tensor_tensor(out=v, in0=th[:, q % 2, :], scalar=1.0, in1=v,
                                                   op0=ALU.add, op1=ALU.mult).then_inc(th_used, 1)
                elif name == "skip" and kind == BWD:
                    dve.wait_ge(K["skip_done"][FWD], 3 * pair + i + 1)
                    halved(dve, "silu", kind, pair, 2 * i + 1)
                    y = yv_of(kind, pair, i)
                    nc.vector.scalar_tensor_tensor(out=y, in0=xs[:, i, :], scalar=sm[:, m_of(i), 6:7], in1=y,
                                                   op0=ALU.mult, op1=ALU.add).then_inc(K["skip_done"][kind], 1)
                elif name == "split_hi":
                    landed(dve, "dbl", kind, pair, i)
                    v = dbl[:, i, :]
                    nc.vector.tensor_tensor(v, v, parts3[:, i, 0, :], ALU.subtract).then_inc(K["hi_done"][kind], 1)
                elif name == "split_lo":
                    dve.wait_ge(K["mid_ready"][kind], 2 * pair + i + 1)
                    nc.vector.tensor_tensor(parts3[:, i, 2, :], dbl[:, i, :], parts3[:, i, 1, :],
                                            ALU.subtract).then_inc(K["lo_done"][kind], 1)

            walk(DVE_ORDER, job, ahead=look_ahead, take_0=lambda g: take_at(g, 0), take_1=lambda g: take_at(g, 1),
                 scan=scan, last=take_last)

        @block.gpsimd
        def _(pool):
            def product(g):
                pool.wait_ge(h_ready, g + 1)
                pool.wait_ge(c_copied, g + 1)
                r = ring[:, g % RING, :]
                nc.gpsimd.tensor_tensor(r, r, c_ring[:, g % C_RING, :], ALU.mult).then_inc(g_ready, 1)

            def job(name, kind, pair, i, unit, use):
                if name == "u":
                    d, u = delta_of(kind, pair, i), u_of(kind, pair, i)
                    pool.wait_ge(K["dt_logged"][kind], 3 * pair + nth(i))
                    nc.gpsimd.tensor_tensor(d, d, u, ALU.add).then_inc(K["dt_added"][kind], 1)
                    pool.wait_ge(K["dt_added"][kind], 3 * pair + nth(i))
                    if kind != ROWS:
                        nc.gpsimd.tensor_tensor(u, d, xs[:, i, :], ALU.mult).then_inc(K["set_ready"][kind], 1)
                        return
                    nc.gpsimd.tensor_tensor(u, d, xs[:, i, :], ALU.mult).then_inc(u_done, 1)
                    pool.wait_ge(u_done, 3 * pair + nth(i))
                    starts = d.rearrange("p (s t) -> p s t", t=W)[:, :, 0:1]
                    nc.gpsimd.memset(starts, BIG).then_inc(K["set_ready"][kind], 1)
                elif name == "gated":
                    pool.wait_ge(y_taken, 2 * (tile_of(kind, pair) + i + 1))
                    halved(pool, "gate", ROWS if kind == ROWS else FWD, pair, 5)
                    y = yv_of(kind, pair, i)
                    nc.gpsimd.tensor_tensor(y, y, sz_of(kind, pair, i), ALU.mult).then_inc(gated_done[kind], 1)
                elif name == "norm":
                    b = i % 2
                    pool.wait_ge(rstd_done, 4 * pair + i + 1)
                    nc.gpsimd.tensor_tensor(x1[:, b, :], x1[:, b, :], squares(b), ALU.mult).then_inc(norm_done, 1)

            def tile_of(kind, pair):
                return TILES * ordinal[kind, pair]

            walk(("product", "jobs"), job, product=product)


def pack(inputs):
    wp = np.zeros((P, NCOL), np.float32)

    def put(name, layer, a, row=0, at=0):
        c = _cols[name, layer][0] + at
        wp[row:row + a.shape[0], c:c + a.shape[1]] = a

    for layer, pre in enumerate(("L0_conv_", "L1_conv_")):
        g = lambda n: np.asarray(inputs[pre + n])
        w_in, w_x, w_dt, w_out = g("W_in"), g("W_x" if layer == 0 else "W_xproj"), g("W_dt"), g("W_out")
        for name, w in (("w_xr", w_in[:, :DI]), ("w_z", w_in[:, DI:])):
            put(name, layer, w[:, :P])
            put(name, layer, w[:, P:], 0, P)
            put(name, layer, w[:, P:], 0, 2 * P + DM)
        bb, cc, dt = w_x[:, RANK:RANK + NS], w_x[:, RANK + NS:], w_x[:, :RANK]
        for b in range(2):
            for at, w in ((NS * b, bb), (NS * (2 + b), cc), (BC_ROWS + RANK * b, dt)):
                put("w_dbl", layer, w[:P], 0, b * X_ROWS + at)
                put("w_dbl", layer, w[P:], b * DM, 2 * X_ROWS + at)
            for q in range(len(DT_TERMS)):
                put("w_dt", layer, w_dt[:, :P], RANK * (2 * q + b), b * P)
                put("w_dt", layer, w_dt[:, P:], RANK * (2 * q + b), 2 * P + b * DM)
        put("w_out", layer, w_out[:P])
        put("w_out", layer, w_out[P:], 0, C)
        put("w_out", layer, w_out[P:], DM, 2 * C)
        rows = np.concatenate([g("conv_w").reshape(DI, TAPS), g("conv_b")[:, None], g("b_dt")[:, None], g("D")[:, None]], axis=1)
        for name, a in (("small", rows), ("a_log", g("A_log"))):
            put(name, layer, a[:P])
            put(name, layer, a[P:], 0, a.shape[1])
            put(name, layer, a[P:], DM, a.shape[1])
        put("ln", None, np.stack([g("ln_g"), g("ln_b")], axis=1), 0, 2 * layer)
    put("ident", None, np.eye(P, dtype=np.float32))
    put("mean", None, np.full((C, C), 1.0 / C, np.float32))
    sel = np.zeros((C, 2, NS), np.float32)
    for b in range(2):
        for g in range(3):
            for n in range(NS):
                sel[(g * 2 + b) * NS + n, b, n] = 1.0
    split = np.zeros((DT_ROWS, 2), np.float32)
    for q, (_, g) in enumerate(DT_TERMS):
        split[2 * RANK * q:2 * RANK * (q + 1)] = (-1.0 if g >= 1 else 0.0, -1.0 if g == 2 else 0.0)
    put("centre", None, np.eye(C, dtype=np.float32) - np.full((C, C), 1.0 / C, np.float32))
    put("sel", None, sel.reshape(C, 2 * NS))
    put("split", None, split)
    return wp


def kernel(**inputs):
    import concourse.bacc as bacc
    from concourse.bass_utils import run_bass_kernel_spmd

    nc = bacc.Bacc("TRN2", target_bir_lowering=False, num_devices=1)
    arrays = {"x": np.ascontiguousarray(np.asarray(inputs["x"]).reshape(B, C, T)), "wpack": pack(inputs)}
    x = nc.dram_tensor("x", (B, C, T), mybir.dt.float32, kind="ExternalInput").ap()
    wpack = nc.dram_tensor("wpack", (P, NCOL), mybir.dt.float32, kind="ExternalInput").ap()
    out = nc.dram_tensor("out", (B, C, T), mybir.dt.float32, kind="ExternalOutput").ap()
    build_program(nc, x, wpack, out)
    r = run_bass_kernel_spmd(nc, [arrays], core_ids=[0])
    return r.results[0]["out"].reshape(B, C, H, W)
```
